# Optimizing a Trainium2 kernel written in Bass

```python
import numpy as np
import jax
import jax.numpy as jnp

def _softmax(x, axis=-1):
    return jax.nn.softmax(x, axis=axis)

def _gelu(x):
    return jax.nn.gelu(x, approximate=True)

def _silu(x):
    return jax.nn.silu(x)

def _sigmoid(x):
    return jax.nn.sigmoid(x)

def _layernorm(x, axis=-1, eps=1e-05):
    m = jnp.mean(x, axis=axis, keepdims=True)
    v = jnp.var(x, axis=axis, keepdims=True)
    return (x - m) / jnp.sqrt(v + eps)

def _scatter_add(tgt, idx, src, axis=0):
    return tgt.at[idx].add(src)

def _segment_sum(src, seg, n):
    return jax.ops.segment_sum(src, seg, n)
kernel_name = 'mk_macaron_d2_jaxref_r8_eb6f60'

def setup_inputs(seed: int=0):
    np.random.seed(seed)
    _w = jnp.asarray

    def _L0_attn_setup():
        import jax, jax.numpy as jnp
        import numpy as np
        B, T, D, H, S = (2, 256, 128, 16, 16)
        HD = D // H
        key = jax.random.key(seed)
        ks = jax.random.split(key, 8)
        x = jax.random.normal(ks[0], (B, T, D), dtype=jnp.float32)
        splat_centers = jax.random.normal(ks[1], (H, S, HD), dtype=jnp.float32) * 0.2
        splat_deltas = jnp.zeros((H, S, HD), dtype=jnp.float32)
        splat_log_scales = jax.random.normal(ks[2], (H, S), dtype=jnp.float32) * 0.2 + np.log(0.5).astype(np.float32)
        splat_log_amplitudes = jax.random.normal(ks[3], (H, S), dtype=jnp.float32) * 0.1 - 0.5
        movement_scale = jnp.asarray(0.08, dtype=jnp.float32)
        temperature = jnp.asarray(1.0, dtype=jnp.float32)
        lim_qkv = 0.5 * np.sqrt(6.0 / (D + 3 * D))
        qkv_w = jax.random.uniform(ks[4], (3 * D, D), dtype=jnp.float32, minval=-lim_qkv, maxval=lim_qkv)
        lim_out = 0.5 * np.sqrt(6.0 / (D + D))
        out_w = jax.random.uniform(ks[5], (D, D), dtype=jnp.float32, minval=-lim_out, maxval=lim_out)
        return {'x': x, 'splat_centers': splat_centers, 'splat_deltas': splat_deltas, 'splat_log_scales': splat_log_scales, 'splat_log_amplitudes': splat_log_amplitudes, 'movement_scale': movement_scale, 'temperature': temperature, 'qkv_w': qkv_w, 'out_w': out_w}
    _L0_attn_in = _L0_attn_setup()

    def _L0_ffn_setup():
        import jax, jax.numpy as jnp
        import numpy as np
        D_MODEL = 128
        D_FF = 512
        N_ZONES = 8
        TOP_K = 3
        ROUTER_H = 32
        BATCH = 16
        SEQ = 256
        key = jax.random.key(seed)
        ks = jax.random.split(key, 8)
        s = lambda *dims: 1.0 / np.sqrt(dims[-2] if len(dims) > 1 else dims[-1])
        x = jax.random.normal(ks[0], (BATCH, SEQ, D_MODEL), dtype=jnp.float32)
        W1 = jax.random.normal(ks[1], (D_MODEL, ROUTER_H), dtype=jnp.float32) / np.sqrt(D_MODEL)
        b1 = jnp.zeros((ROUTER_H,), dtype=jnp.float32)
        W2 = jax.random.normal(ks[2], (ROUTER_H, N_ZONES), dtype=jnp.float32) / np.sqrt(ROUTER_H)
        b2 = jnp.zeros((N_ZONES,), dtype=jnp.float32)
        Wa = jax.random.normal(ks[3], (N_ZONES, D_MODEL, D_FF), dtype=jnp.float32) / np.sqrt(D_MODEL)
        Wb = jax.random.normal(ks[4], (N_ZONES, D_FF, D_MODEL), dtype=jnp.float32) / np.sqrt(D_FF)
        return {'x': x, 'W1': W1, 'b1': b1, 'W2': W2, 'b2': b2, 'Wa': Wa, 'Wb': Wb}
    _L0_ffn_in = _L0_ffn_setup()

    def _L1_attn_setup():
        import jax, jax.numpy as jnp
        import numpy as np
        import math
        DK = 128
        key = jax.random.key(seed)
        k1, k2 = jax.random.split(key)
        x = jax.random.normal(k1, (4, 256, 128), dtype=jnp.float32)
        W = jax.random.normal(k2, (128, 3 * DK), dtype=jnp.float32) * (1.0 / math.sqrt(128))
        b = jnp.zeros((3 * DK,), dtype=jnp.float32)
        return {'x': x, 'W': W, 'b': b}
    _L1_attn_in = _L1_attn_setup()

    def _L1_ffn_setup():
        import jax, jax.numpy as jnp
        import numpy as np
        D_MODEL = 128
        M = 64
        INNER = 16
        key = jax.random.key(seed)
        ks = jax.random.split(key, 9)

        def init(k, shape, fan_in):
            bound = 1.0 / np.sqrt(fan_in)
            return jax.random.uniform(k, shape, jnp.float32, -bound, bound)
        x = jax.random.normal(ks[0], (16, 512, D_MODEL), dtype=jnp.float32)
        Win = init(ks[1], (D_MODEL, M), D_MODEL)
        bin_ = init(ks[2], (M,), D_MODEL)
        W1 = init(ks[3], (M, INNER), 1)
        b1 = init(ks[4], (M, INNER), 1)
        W2 = init(ks[5], (M, INNER), INNER)
        b2 = init(ks[6], (M,), INNER)
        Wout = init(ks[7], (M, D_MODEL), M)
        bout = init(ks[8], (D_MODEL,), M)
        return {'x': x, 'Win': Win, 'bin_': bin_, 'W1': W1, 'b1': b1, 'W2': W2, 'b2': b2, 'Wout': Wout, 'bout': bout}
    _L1_ffn_in = _L1_ffn_setup()
    _d = {'L0_attn_x': _L0_attn_in['x'], 'L0_attn_splat_centers': _L0_attn_in['splat_centers'], 'L0_attn_splat_deltas': _L0_attn_in['splat_deltas'], 'L0_attn_splat_log_scales': _L0_attn_in['splat_log_scales'], 'L0_attn_splat_log_amplitudes': _L0_attn_in['splat_log_amplitudes'], 'L0_attn_movement_scale': _L0_attn_in['movement_scale'], 'L0_attn_temperature': _L0_attn_in['temperature'], 'L0_attn_qkv_w': _L0_attn_in['qkv_w'], 'L0_attn_out_w': _L0_attn_in['out_w'], 'L0_ffn_W1': _L0_ffn_in['W1'], 'L0_ffn_b1': _L0_ffn_in['b1'], 'L0_ffn_W2': _L0_ffn_in['W2'], 'L0_ffn_b2': _L0_ffn_in['b2'], 'L0_ffn_Wa': _L0_ffn_in['Wa'], 'L0_ffn_Wb': _L0_ffn_in['Wb'], 'L1_attn_W': _L1_attn_in['W'], 'L1_attn_b': _L1_attn_in['b'], 'L1_ffn_Win': _L1_ffn_in['Win'], 'L1_ffn_bin_': _L1_ffn_in['bin_'], 'L1_ffn_W1': _L1_ffn_in['W1'], 'L1_ffn_b1': _L1_ffn_in['b1'], 'L1_ffn_W2': _L1_ffn_in['W2'], 'L1_ffn_b2': _L1_ffn_in['b2'], 'L1_ffn_Wout': _L1_ffn_in['Wout'], 'L1_ffn_bout': _L1_ffn_in['bout']}
    _x0 = _d['L0_attn_x']
    _d['L0_attn_x'] = jax.random.normal(jax.random.fold_in(jax.random.key(seed), 1), (32, 256, 128), dtype=_x0.dtype)
    del _x0
    return _d

def reference(L0_attn_x, L0_attn_splat_centers, L0_attn_splat_deltas, L0_attn_splat_log_scales, L0_attn_splat_log_amplitudes, L0_attn_movement_scale, L0_attn_temperature, L0_attn_qkv_w, L0_attn_out_w, L0_ffn_W1, L0_ffn_b1, L0_ffn_W2, L0_ffn_b2, L0_ffn_Wa, L0_ffn_Wb, L1_attn_W, L1_attn_b, L1_ffn_Win, L1_ffn_bin_, L1_ffn_W1, L1_ffn_b1, L1_ffn_W2, L1_ffn_b2, L1_ffn_Wout, L1_ffn_bout):

    def _L0_attn_ref(x, splat_centers, splat_deltas, splat_log_scales, splat_log_amplitudes, movement_scale, temperature, qkv_w, out_w):
        import jax, jax.numpy as jnp
        import numpy as np
        B, T, D, H, S = (2, 256, 128, 16, 16)
        HD = D // H
        Bx, Tx, Dx = x.shape
        Hx, Sx, hd = splat_centers.shape
        qkv = (x @ qkv_w.T).reshape(Bx, Tx, 3, Hx, hd)
        q, k, v = (qkv[:, :, 0], qkv[:, :, 1], qkv[:, :, 2])
        centers = splat_centers + splat_deltas * jax.nn.sigmoid(movement_scale) * 0.2
        scales = jnp.clip(jnp.exp(splat_log_scales), 0.01, 2.0)
        amplitudes = jnp.clip(jnp.exp(splat_log_amplitudes), 1e-06, 10.0)
        inv_var = -0.5 / (scales ** 2 + 1e-08)
        q_dists = jnp.sum((q[:, :, :, None, :] - centers[None, None]) ** 2, axis=-1)
        k_dists = jnp.sum((k[:, :, :, None, :] - centers[None, None]) ** 2, axis=-1)
        q_weights = jnp.exp(q_dists * inv_var)
        k_weights = jnp.exp(k_dists * inv_var)
        logits = jnp.einsum('bihs,bjhs,hs->bijh', q_weights, k_weights, amplitudes)
        temp = jnp.clip(temperature, 0.1, 10.0)
        attention = jax.nn.softmax(logits / temp, axis=2)
        out = jnp.einsum('bijh,bjhd->bihd', attention, v).reshape(Bx, Tx, Dx)
        return out @ out_w.T

    def _L0_ffn_ref(x, W1, b1, W2, b2, Wa, Wb):
        import jax, jax.numpy as jnp
        import numpy as np
        D_MODEL = 128
        D_FF = 512
        N_ZONES = 8
        TOP_K = 3
        ROUTER_H = 32
        BATCH = 16
        SEQ = 256
        pooled = x.mean(axis=1)
        h = jnp.tanh(pooled @ W1 + b1)
        logits = h @ W2 + b2
        probs = jax.nn.softmax(logits, axis=-1)
        top_p, top_i = jax.lax.top_k(probs, TOP_K)
        top_w = top_p / top_p.sum(axis=-1, keepdims=True)
        onehot = jax.nn.one_hot(top_i, N_ZONES, dtype=x.dtype)
        w = jnp.einsum('bk,bke->be', top_w, onehot)
        zone_outputs = jnp.zeros_like(x)
        for e in range(N_ZONES):
            z = jax.nn.gelu(x @ Wa[e]) @ Wb[e]
            zone_outputs = zone_outputs + z * w[:, e, None, None]
        return x + zone_outputs

    def _L1_attn_ref(x, W, b):
        import jax, jax.numpy as jnp
        import numpy as np
        import math
        DK = 128
        qkv = jnp.einsum('btc,cd->btd', x, W) + b
        q, k, v = jnp.split(qkv, 3, axis=-1)
        scale = 1.0 / math.sqrt(DK)
        weights = jnp.einsum('btc,bTc->btT', q, k) * scale
        T = weights.shape[-1]
        mask = jnp.tril(jnp.ones((T, T), dtype=jnp.float32))
        logits = jnp.where(mask == 0, jnp.float32(-9000000000000000.0), weights)
        attention = jax.nn.softmax(logits, axis=-1)
        values = jnp.einsum('btT,bTc->btc', attention, v)
        return values

    def _L1_ffn_ref(x, Win, bin_, W1, b1, W2, b2, Wout, bout):
        import jax, jax.numpy as jnp
        import numpy as np
        D_MODEL = 128
        M = 64
        INNER = 16
        s = jnp.einsum('btd,dm->btm', x, Win) + bin_
        h = jax.nn.relu(s[..., None] * W1 + b1)
        g = jnp.einsum('btmh,mh->btm', h, W2) + b2
        out = jnp.einsum('btm,md->btd', g, Wout) + bout
        return out
    x = L0_attn_x
    x = x + 0.5 * _L0_ffn_ref(_layernorm(x, axis=-1), L0_ffn_W1, L0_ffn_b1, L0_ffn_W2, L0_ffn_b2, L0_ffn_Wa, L0_ffn_Wb)
    x = x + _L0_attn_ref(_layernorm(x, axis=-1), L0_attn_splat_centers, L0_attn_splat_deltas, L0_attn_splat_log_scales, L0_attn_splat_log_amplitudes, L0_attn_movement_scale, L0_attn_temperature, L0_attn_qkv_w, L0_attn_out_w)
    x = x + 0.5 * _L0_ffn_ref(_layernorm(x, axis=-1), L0_ffn_W1, L0_ffn_b1, L0_ffn_W2, L0_ffn_b2, L0_ffn_Wa, L0_ffn_Wb)
    x = x + 0.5 * _L1_ffn_ref(_layernorm(x, axis=-1), L1_ffn_Win, L1_ffn_bin_, L1_ffn_W1, L1_ffn_b1, L1_ffn_W2, L1_ffn_b2, L1_ffn_Wout, L1_ffn_bout)
    x = x + _L1_attn_ref(_layernorm(x, axis=-1), L1_attn_W, L1_attn_b)
    x = x + 0.5 * _L1_ffn_ref(_layernorm(x, axis=-1), L1_ffn_Win, L1_ffn_bin_, L1_ffn_W1, L1_ffn_b1, L1_ffn_W2, L1_ffn_b2, L1_ffn_Wout, L1_ffn_bout)
    return x

_drawn_inputs = setup_inputs


def setup_inputs(seed=0):
    import zlib

    import numpy as np

    out = dict(_drawn_inputs(seed))
    spreads = {'L0_attn_splat_deltas': (0.0, 0.8),
     'L0_ffn_b1': (0.0, 0.1),
     'L0_ffn_b2': (0.0, 0.1),
     'L1_attn_b': (0.0, 0.1)}
    factors = {'L0_attn_splat_centers': 8.0,
     'L0_attn_splat_log_scales': 8.0,
     'L0_attn_splat_log_amplitudes': 8.0,
     'L0_attn_qkv_w': 3.462,
     'L0_attn_out_w': 3.573,
     'L1_ffn_bin_': 8.0}
    for name, (base, spread) in spreads.items():
        noise = np.random.default_rng([zlib.crc32(name.encode()), seed]).standard_normal(out[name].shape)
        drawn = base * np.exp(spread * noise) if base else spread * noise
        out[name] = jnp.asarray(drawn.astype(out[name].dtype))
    for name, factor in factors.items():
        out[name] = (out[name] * factor).astype(out[name].dtype)
    return out
```

```python
import math
from contextlib import ExitStack

import concourse.bass as bass
from concourse import mybir

F32 = mybir.dt.float32
F16 = mybir.dt.float16
I32 = mybir.dt.int32
U32 = mybir.dt.uint32
ALU = mybir.AluOpType
ACT = mybir.ActivationFunctionType
AX = mybir.AxisListType

P = 128
SAMPLES = 32
TOKENS = 256
TILES = TOKENS // P
EPS = 1e-5

ZONES, ZONE_HIDDEN, TOP_K, ROUTER_H = 8, 512, 3, 32
CHUNKS = ZONE_HIDDEN // P
UNITS = SAMPLES * TOP_K
WEIGHT_SHIFT = 2.0 ** 8
HIDDEN_SHIFT = 2.0 ** 6

HEADS, SPLATS, HEAD_DIM = 16, 16, 8
GROUP = 32
HEAD_GROUPS = P // GROUP
FTILES = HEADS // HEAD_GROUPS
HEAD_UNITS = HEADS // 2
MAX_FILLS = TILES * HEAD_UNITS

SPLINES, KNOTS = 64, 16
HALF_KNOTS = KNOTS // 2
MASKED = -9000000000000000.0


def wait(engine, semaphore, value):
    if isinstance(value, int) and value <= 0:
        return
    engine.wait_ge(semaphore, value)


def pairs(engine, first, end):
    return engine.Fori(first, end - 1, 2)


class Chain:

    def __init__(self, engine, semaphore, base=0):
        self.engine, self.semaphore, self.base, self.n = engine, semaphore, base, 0

    def __call__(self, instruction):
        self.n += 1
        instruction.then_inc(self.semaphore, 1)
        self.engine.wait_ge(self.semaphore, self.base + self.n)


def tile_of(x_res, sample, tile=None):
    if isinstance(sample, int):
        rows = x_res[:, TILES * sample:TILES * (sample + 1), :]
    else:
        rows = x_res[:, bass.ds(sample * TILES, TILES), :]
    return rows if tile is None else rows[:, tile, :]


class RowNorm:

    def __init__(self, nc, s, ctx, stage, buffers):
        sb, sem = sb_maker(nc, ctx), sem_maker(nc, ctx, stage)
        self.nc, self.s = nc, s
        self.stats = sb(stage + "_stats", [P, TILES, 6], F32)
        self.moments = [sb(f"{stage}_moments{i}", [P, TILES, 2], F32) for i in range(2)]
        self.shifted = sb(stage + "_shifted", [P, TILES], F32)
        self.rstd = [sb(f"{stage}_rstd{i}", [P, TILES], F32) for i in range(2)]
        self.out = [sb(f"{stage}_normed{i}", [P, TILES, P], F32) for i in range(buffers)]
        self.stats_ready, self.moments_ready, self.shifted_ready, self.rstd_ready, self.ready = (
            sem(n) for n in ("stats_ready", "moments_ready", "shifted_ready", "rstd_ready", "norm_ready"))

    def statistics(self, dve, b, parity):
        wait(dve, self.moments_ready, b)
        for t in range(TILES):
            last = self.nc.vector.bn_stats(self.stats[:, t, :], tile_of(self.s.x_res, b, t))
        last.then_inc(self.stats_ready, 1)
        value = b + 1 if isinstance(b, int) else dve.to_reg(b + 1)
        dve.wait_ge(self.stats_ready, 1)
        dve.wait_ge(self.stats_ready, value)
        for t in range(TILES):
            last = self.nc.vector.bn_aggr(self.moments[parity][:, t, :], self.stats[:, t, :])
        last.then_inc(self.moments_ready, 1)

    def powers(self, pool, after=None):
        def power(b, parity):
            pool.wait_ge(self.moments_ready, b + 1)
            wait(pool, self.rstd_ready, b)
            self.nc.gpsimd.tensor_tensor(self.shifted[:, :], self.moments[parity][:, :, 1], self.s.eps[:, :],
                                         ALU.add).then_inc(self.shifted_ready, 1)
            pool.wait_ge(self.shifted_ready, b + 1)
            wait(pool, self.ready, b - 1)
            self.nc.gpsimd.tensor_tensor(self.rstd[parity][:, :], self.shifted[:, :], self.s.minus_half[:, :],
                                         ALU.pow).then_inc(self.rstd_ready, 1)

        power(0, 0)
        power(1, 1)
        if after is not None:
            after(0)
        with pairs(pool, 2, SAMPLES) as i:
            for parity in range(2):
                power(i + parity, parity)
                if after is not None:
                    after(i + parity - 1)
        if after is not None:
            after(SAMPLES - 1)

    def apply(self, dve, b, parity, out):
        dve.wait_ge(self.rstd_ready, b + 1)
        for t in range(TILES):
            last = self.nc.vector.tensor_scalar(out[:, t, :], tile_of(self.s.x_res, b, t),
                                                self.moments[parity][:, t, 0:1], self.rstd[parity][:, t:t + 1],
                                                ALU.subtract, ALU.mult)
        last.then_inc(self.ready, 1)


class Store:
    pass


def sb_maker(nc, ctx):
    return lambda name, shape, dt: ctx.enter_context(nc.sbuf_tensor(name, shape, dt))


def ps_maker(nc, ctx):
    return lambda name, shape: ctx.enter_context(nc.psum_tensor(name, shape, F32))


def sem_maker(nc, ctx, stage):
    return lambda name: ctx.enter_context(nc.semaphore(f"{stage}_{name}"))


def load_and_constants(nc, s, a):
    with ExitStack() as ctx:
        sem = sem_maker(nc, ctx, "load")
        loads = []

        def load(dst, src):
            loads.append((dst, src))

        load(s.stage_a[:, :].rearrange("d (e f) -> d e f", e=ZONES), a["L0_ffn_Wa"].rearrange("e d f -> d e f"))
        load(s.stage_b[:, :].rearrange("f (e c d) -> f e c d", e=ZONES, c=CHUNKS),
             a["L0_ffn_Wb"].rearrange("e (c f) d -> f e c d", f=P))
        load(s.x_res[:, :, :], a["L0_attn_x"].rearrange("b (t p) d -> p (b t) d", p=P))
        load(s.qkv_rows[:, :, :], a["L0_attn_qkv_w"].rearrange("(k o) d -> o k d", o=P))
        load(s.out_rows[:, :], a["L0_attn_out_w"])
        load(s.router_w1[:, :], a["L0_ffn_W1"])
        load(s.router_w2[:, :], a["L0_ffn_W2"])
        load(s.router_b1[:, :], a["L0_ffn_b1"].unsqueeze(1))
        load(s.router_b2[:, :], a["L0_ffn_b2"].unsqueeze(0))
        for h in range(HEADS):
            rows = slice(h * HEAD_DIM, (h + 1) * HEAD_DIM)
            load(s.centers[rows, :], a["L0_attn_splat_centers"][h].rearrange("s d -> d s"))
            load(s.deltas[rows, :], a["L0_attn_splat_deltas"][h].rearrange("s d -> d s"))
            load(s.log_scales[rows, :], a["L0_attn_splat_log_scales"][h].partition_broadcast(HEAD_DIM))
            load(s.log_amps[rows, :], a["L0_attn_splat_log_amplitudes"][h].partition_broadcast(HEAD_DIM))
        load(s.movement[:, :], a["L0_attn_movement_scale"].partition_broadcast(P).unsqueeze(1))
        load(s.temperature[:, :], a["L0_attn_temperature"].partition_broadcast(P).unsqueeze(1))
        load(s.attn1_w[:, :], a["L1_attn_W"])
        bias = a["L1_attn_b"]
        for k in range(2):
            load(s.attn1_bqk[:, k:k + 1], bias[k * P:(k + 1) * P].unsqueeze(1))
        load(s.attn1_bv[:, :], bias[2 * P:3 * P].partition_broadcast(P))
        for c in range(2):
            half = slice(c * SPLINES, (c + 1) * SPLINES)
            knots = slice(c * HALF_KNOTS, (c + 1) * HALF_KNOTS)
            load(s.win2[:, half], a["L1_ffn_Win"])
            load(s.bin2[half, :], a["L1_ffn_bin_"].unsqueeze(1))
            load(s.relu_scale[half, :], a["L1_ffn_W1"][:, knots])
            load(s.knot_b1[half, :], a["L1_ffn_b1"][:, knots])
            load(s.knot_w2[half, :], a["L1_ffn_W2"][:, knots])
            load(s.wout2[half, :], a["L1_ffn_Wout"])
        load(s.b2_col[:, :], a["L1_ffn_b2"].unsqueeze(1))
        load(s.bout_row[:, :], a["L1_ffn_bout"].unsqueeze(0))
        loaded = sem("loaded")
        zeroed = sem("zeroed")

        with nc.Block() as block:
            @block.sync
            def _(sp):
                for dst, src in loads:
                    sp.dma_start(dst, src, allow_slow_non_contiguous=True).then_inc(loaded, 16)
                sp.wait_ge(loaded, 16 * len(loads))

            @block.gpsimd
            def _(pool):
                nc.gpsimd.memset(s.ident32[:, :], 0.0)
                nc.gpsimd.memset(s.ident16[:, :], 0.0)
                nc.gpsimd.memset(s.causal[:, :], 0.0).then_inc(zeroed, 1)
                pool.wait_ge(zeroed, 1)
                for m in (s.ident32, s.ident16):
                    nc.gpsimd.affine_select(out=m[:, :], in_=m[:, :], compare_op=ALU.not_equal, fill=1.0,
                                            base=0, pattern=[[-1, P]], channel_multiplier=1)
                for c in (0, 2):
                    part = s.causal[:, c * P:(c + 1) * P]
                    nc.gpsimd.affine_select(out=part, in_=part, compare_op=ALU.is_ge, fill=MASKED,
                                            base=0, pattern=[[-1, P]], channel_multiplier=1)
                nc.gpsimd.iota(s.row_index[:, :], pattern=[[0, 1]], base=0, channel_multiplier=1)

            @block.vector
            def _(dve):
                nc.vector.memset(s.ones_row[:, :], 1.0)
                nc.vector.memset(s.eps[:, :], EPS)
                nc.vector.memset(s.minus_half[:, :], -0.5)
                nc.vector.memset(s.neg_max[:, :, :, :], 0.0)
                nc.vector.memset(s.values[:, :, :, :, :], 1.0)


def prepare_zones(nc, s):
    with ExitStack() as ctx:
        sb, ps, sem = sb_maker(nc, ctx), ps_maker(nc, ctx), sem_maker(nc, ctx, "zonew")
        row_max = sb("zonew_row_max", [P, 2], F32)
        all_max = sb("zonew_all_max", [1, 2], F32)
        power = sb("zonew_power", [1, 2], F32)
        powers = sb("zonew_powers", [P, 2], F32)
        inverse = sb("zonew_inverse", [P, 2], F32)
        scale = sb("zonew_scale", [P, 2], F32)
        spread = ps("zonew_spread", [P, 512])
        maxima, turned, power_ready, spread_ready, links = (
            sem(n) for n in ("maxima", "turned", "power_ready", "spread_ready", "links"))

        with nc.Block() as block:
            @block.vector
            def _(dve):
                link = Chain(dve, links)
                for k, w in enumerate((s.stage_a, s.stage_b)):
                    last = nc.vector.tensor_reduce(row_max[:, k:k + 1], w[:, :], AX.X, ALU.max,
                                                   apply_absolute_value=True)
                last.then_inc(maxima, 1)
                dve.wait_ge(turned, 1)
                link(nc.vector.tensor_reduce(all_max[:, :], spread[0:1, 0:2 * P].rearrange("a (k p) -> a k p", k=2),
                                             AX.X, ALU.max))
                link(nc.vector.tensor_scalar_max(all_max[:, :], all_max[:, :], 1e-30))
                nc.vector.tensor_scalar(power[:, :].bitcast(I32), all_max[:, :].bitcast(I32), 0x7F800000, None,
                                        ALU.bitwise_and).then_inc(power_ready, 1)
                dve.wait_ge(spread_ready, 1)
                link(nc.vector.tensor_copy(powers[:, :], spread[:, 0:2]))
                link(nc.vector.reciprocal(inverse[:, :], powers[:, :]))
                link(nc.vector.tensor_scalar_mul(scale[:, :], inverse[:, :], WEIGHT_SHIFT))
                nc.vector.tensor_scalar_mul(s.gelu_scale[:, :], powers[:, 0:1], 1.0 / WEIGHT_SHIFT)
                nc.vector.tensor_scalar_mul(s.hidden_scale[:, :], inverse[:, 0:1], HIDDEN_SHIFT)
                nc.vector.scalar_tensor_tensor(s.zone_out_scale[:, :], powers[:, 0:1],
                                               0.5 / (HIDDEN_SHIFT * WEIGHT_SHIFT), powers[:, 1:2],
                                               ALU.mult, ALU.mult)
                for k, (w, hi, lo) in enumerate(((s.stage_a, s.wa_hi, s.wa_lo), (s.stage_b, s.wb_hi, s.wb_lo))):
                    link(nc.vector.tensor_scalar(hi[:, :], w[:, :], scale[:, k:k + 1], None, ALU.mult))
                    nc.vector.scalar_tensor_tensor(lo[:, :], w[:, :], scale[:, k:k + 1], hi[:, :],
                                                   ALU.mult, ALU.subtract)

            @block.tensor
            def _(pe):
                pe.wait_ge(maxima, 1)
                for k in range(2):
                    last = nc.tensor.matmul(spread[0:1, k * P:(k + 1) * P], row_max[:, k:k + 1], s.ident32[:, :],
                                            start=True, stop=True)
                last.then_inc(turned, 1)
                pe.wait_ge(power_ready, 1)
                nc.tensor.matmul(spread[:, 0:2], s.ones_row[:, :], power[:, :],
                                 start=True, stop=True).then_inc(spread_ready, 1)


def prepare_splats(nc, s):
    with ExitStack() as ctx:
        sb, ps, sem = sb_maker(nc, ctx), ps_maker(nc, ctx), sem_maker(nc, ctx, "splatw")
        bits = sb("splatw_bits", [P, 4], I32)
        index = sb("splatw_index", [P, 4], F32)
        in_group = sb("splatw_in_group", [P, HEAD_GROUPS], F32)
        in_tile = sb("splatw_in_tile", [P, FTILES], F32)
        sig = sb("splatw_sig", [P, 1], F32)
        log_temp = sb("splatw_log_temp", [P, 1], F32)
        temp = sb("splatw_temp", [P, 1], F32)
        c = sb("splatw_c", [P, SPLATS], F32)
        var = sb("splatw_var", [P, SPLATS], F32)
        scales = sb("splatw_scales", [P, SPLATS], F32)
        small = sb("splatw_small", [P, 4, SPLATS], F32)
        wide = sb("splatw_wide", [P, 4, HEAD_GROUPS, 2, SPLATS], F32)
        turned = ps("splatw_turned", [P, 4 * P])
        consts = ps("splatw_consts", [P, 2 * FTILES])
        (transposed, act_done, temp_ready, links, wide_ready, consts_ready, moved) = (
            sem(n) for n in ("transposed", "act_done", "temp_ready", "links", "wide_ready", "consts_ready", "moved"))
        LINEAR, SQUARE, KEY_CONST, QUERY_CONST = range(4)

        with nc.Block() as block:
            @block.tensor
            def _(pe):
                for k in range(3):
                    nc.tensor.transpose(turned[:, k * P:(k + 1) * P], s.qkv_rows[:, k, :], s.ident32[:, :])
                nc.tensor.transpose(turned[:, 3 * P:4 * P], s.out_rows[:, :], s.ident32[:, :]).then_inc(transposed, 1)
                pe.wait_ge(wide_ready, 1)
                for k, kind in enumerate((QUERY_CONST, KEY_CONST)):
                    last = nc.tensor.matmul(consts[:, k * FTILES:(k + 1) * FTILES],
                                            wide[:, kind, :, :, :].rearrange("p g r s -> p (g r s)"),
                                            in_tile[:, :], start=True, stop=True)
                last.then_inc(consts_ready, 1)

            @block.scalar
            def _(act):
                nc.scalar.activation(scales[:, :], s.log_scales[:, :], ACT.Exp).then_inc(act_done, 1)
                nc.scalar.activation(sig[:, :], s.movement[:, :], ACT.Sigmoid).then_inc(act_done, 1)
                act.wait_ge(temp_ready, 1)
                nc.scalar.activation(log_temp[:, :], temp[:, :], ACT.Ln).then_inc(act_done, 1)

            @block.vector
            def _(dve):
                link = Chain(dve, links)
                nc.vector.tensor_scalar(temp[:, :], s.temperature[:, :], 0.1, 10.0,
                                        ALU.max, ALU.min).then_inc(temp_ready, 1)
                link(nc.vector.tensor_scalar(bits[:, 0:1], s.row_index[:, :], 3, 3,
                                             ALU.arith_shift_right, ALU.bitwise_and))
                link(nc.vector.tensor_scalar(bits[:, 1:2], s.row_index[:, :], 5, 3,
                                             ALU.arith_shift_right, ALU.bitwise_and))
                link(nc.vector.tensor_scalar(bits[:, 2:3], s.row_index[:, :], GROUP - 1, None, ALU.bitwise_and))
                link(nc.vector.tensor_scalar(bits[:, 3:4], s.row_index[:, :], 2 * GROUP - 1, None, ALU.bitwise_and))
                link(nc.vector.tensor_copy(index[:, :], bits[:, :]))
                for g in range(HEAD_GROUPS):
                    nc.vector.tensor_scalar(in_group[:, g:g + 1], index[:, 0:1], float(g), None, ALU.is_equal)
                    nc.vector.tensor_scalar(in_tile[:, g:g + 1], index[:, 1:2], float(g), None, ALU.is_equal)
                nc.vector.tensor_scalar(s.first_copy[:, :], index[:, 2:3], float(SPLATS), None, ALU.is_lt)
                nc.vector.tensor_scalar(s.minus_second[:, :], index[:, 2:3], float(SPLATS), -1.0, ALU.is_ge, ALU.mult)
                nc.vector.tensor_scalar(s.shift_row[:, :], index[:, 2:3], float(SPLATS), None, ALU.is_equal)
                nc.vector.tensor_scalar(s.linear_rows[:, :], index[:, 3:4], float(GROUP), None, ALU.is_lt)
                link(nc.vector.tensor_scalar(s.square_rows[:, :], index[:, 3:4], float(GROUP), None, ALU.is_ge))
                dve.wait_ge(act_done, 2)
                link(nc.vector.tensor_scalar(c[:, :], s.deltas[:, :], sig[:, :], 0.2, ALU.mult, ALU.mult))
                link(nc.vector.tensor_tensor(c[:, :], c[:, :], s.centers[:, :], ALU.add))
                link(nc.vector.tensor_scalar(scales[:, :], scales[:, :], 0.01, 2.0, ALU.max, ALU.min))
                link(nc.vector.tensor_tensor(var[:, :], scales[:, :], scales[:, :], ALU.mult))
                link(nc.vector.tensor_scalar_add(var[:, :], var[:, :], 1e-8))
                link(nc.vector.reciprocal(var[:, :], var[:, :]))
                link(nc.vector.tensor_scalar_mul(small[:, SQUARE, :], var[:, :], -0.5))
                link(nc.vector.scalar_tensor_tensor(small[:, LINEAR, :], c[:, :], -2.0, small[:, SQUARE, :],
                                                    ALU.mult, ALU.mult))
                link(nc.vector.scalar_tensor_tensor(small[:, KEY_CONST, :], small[:, LINEAR, :], -0.5, c[:, :],
                                                    ALU.mult, ALU.mult))
                dve.wait_ge(act_done, 3)
                link(nc.vector.tensor_scalar(scales[:, :], s.log_amps[:, :], math.log(1e-6), math.log(10.0),
                                             ALU.max, ALU.min))
                link(nc.vector.tensor_scalar(scales[:, :], scales[:, :], log_temp[:, :], 1.0 / HEAD_DIM,
                                             ALU.subtract, ALU.mult))
                link(nc.vector.tensor_tensor(small[:, QUERY_CONST, :], scales[:, :], small[:, KEY_CONST, :], ALU.add))
                for g in range(HEAD_GROUPS):
                    for copy in range(2):
                        last = nc.vector.tensor_scalar(wide[:, :, g, copy, :], small[:, :, :], in_group[:, g:g + 1],
                                                       None, ALU.mult)
                last.then_inc(wide_ready, 1)
                dve.wait_ge(transposed, 1)
                for k, w in enumerate((s.wq_pairs, s.wk_pairs)):
                    src = turned[:, k * P:(k + 1) * P].rearrange("d (t c) -> d t c", t=FTILES)
                    for copy in range(2):
                        nc.vector.tensor_copy(w[:, :, copy, :], src)
                nc.vector.tensor_copy(s.wv[:, :], turned[:, 2 * P:3 * P])
                nc.vector.tensor_copy(s.wo[:, :], turned[:, 3 * P:4 * P])
                dve.wait_ge(consts_ready, 1)
                nc.vector.tensor_copy(s.feature_bias[:, :], consts[:, :])

            @block.sync
            def _(sp):
                sp.wait_ge(wide_ready, 1)
                n = 0
                for t in range(FTILES):
                    rows = slice(t * GROUP, (t + 1) * GROUP)
                    for k, kind in enumerate((LINEAR, SQUARE)):
                        to = 2 * GROUP * (t % 2) + GROUP * k
                        sp.dma_start(s.feature_w[to:to + GROUP, t // 2, :],
                                     wide[rows, kind, :, :, :].rearrange("p g r s -> p (g r s)")).then_inc(moved, 16)
                        n += 16
                sp.wait_ge(moved, n)


def prepare_splines(nc, s):
    with ExitStack() as ctx:
        sb, ps, sem = sb_maker(nc, ctx), ps_maker(nc, ctx), sem_maker(nc, ctx, "splinew")
        scaled = sb("splinew_scaled", [P, HALF_KNOTS], F32)
        half_row = sb("splinew_half_row", [1, P], F32)
        half_b2 = sb("splinew_half_b2", [SPLINES, P], F32)
        out_bias = ps("splinew_out_bias", [P, P])
        links, rows_ready, bias_ready = (sem(n) for n in ("links", "rows_ready", "bias_ready"))

        with nc.Block() as block:
            @block.vector
            def _(dve):
                link = Chain(dve, links)
                link(nc.vector.tensor_scalar(scaled[:, :], s.relu_scale[:, :], s.bin2[:, :], None, ALU.mult))
                nc.vector.tensor_tensor(s.relu_bias[:, :], scaled[:, :], s.knot_b1[:, :], ALU.add)
                for k in range(HALF_KNOTS):
                    nc.vector.tensor_scalar(s.knot_out[:, k, :], s.wout2[:, :], s.knot_w2[:, k:k + 1], 0.5,
                                            ALU.mult, ALU.mult)
                link(nc.vector.memset(half_b2[:, :], 0.5))
                nc.vector.tensor_scalar_mul(half_row[:, :], s.bout_row[:, :], 0.5)
                nc.vector.tensor_scalar(half_b2[:, :], half_b2[:, :], s.b2_col[:, :], None,
                                        ALU.mult).then_inc(rows_ready, 1)
                dve.wait_ge(bias_ready, 1)
                nc.vector.tensor_copy(s.half_bias[:, 0, :], out_bias[:, :])
                nc.vector.tensor_copy(s.half_bias[:, 1, :], out_bias[:, :])

            @block.tensor
            def _(pe):
                pe.wait_ge(rows_ready, 1)
                nc.tensor.matmul(out_bias[:, :], half_b2[:, :], s.wout2[0:SPLINES, :], start=True, stop=False)
                nc.tensor.matmul(out_bias[:, :], s.ones_row[:, :], half_row[:, :],
                                 start=False, stop=True).then_inc(bias_ready, 1)


def zone_norm(nc, s, stage):
    with ExitStack() as ctx:
        sb, ps, sem = sb_maker(nc, ctx), ps_maker(nc, ctx), sem_maker(nc, ctx, stage)
        norm = RowNorm(nc, s, ctx, stage, 2)
        normed, norm_ready = norm.out, norm.ready
        turned = [ps(f"{stage}_turned{i}", [P, 512]) for i in range(2)]
        turned_ready, high_ready, parts_ready = (
            sem(n) for n in ("turned_ready", "high_ready", "parts_ready"))

        with nc.Block() as block:
            @block.vector
            def _(dve):
                def apply(b, parity):
                    wait(dve, turned_ready, b - 1)
                    norm.apply(dve, b, parity, normed[parity])
                    dve.wait_ge(norm_ready, b + 1)
                    rows = tile_of(s.x_res, b)
                    nc.vector.scalar_tensor_tensor(rows, normed[parity][:, :, :], 0.5, rows, ALU.mult, ALU.add)

                def low(b, parity):
                    dve.wait_ge(high_ready, b + 1)
                    nc.vector.tensor_tensor(s.norm_lo[:, bass.ds(b, 1), :], turned[parity][:, 0:TOKENS],
                                            s.norm_hi[:, bass.ds(b, 1), :], ALU.subtract).then_inc(parts_ready, 1)

                norm.statistics(dve, 0, 0)
                norm.statistics(dve, 1, 1)
                apply(0, 0)
                with pairs(dve, 1, SAMPLES - 1) as i:
                    for step, parity in ((0, 1), (1, 0)):
                        norm.statistics(dve, i + step + 1, 1 - parity)
                        apply(i + step, parity)
                        low(i + step - 1, 1 - parity)
                apply(SAMPLES - 1, 1)
                low(SAMPLES - 2, 0)
                low(SAMPLES - 1, 1)

            @block.gpsimd
            def _(pool):
                norm.powers(pool)

            @block.tensor
            def _(pe):
                def transpose(b, parity):
                    pe.wait_ge(norm_ready, b + 1)
                    wait(pe, parts_ready, b - 1)
                    for t in range(TILES):
                        last = nc.tensor.transpose(turned[parity][:, t * P:(t + 1) * P],
                                                   normed[parity][:, t, :], s.ident32[:, :])
                    last.then_inc(turned_ready, 1)

                transpose(0, 0)
                transpose(1, 1)
                with pairs(pe, 2, SAMPLES) as i:
                    for parity in range(2):
                        transpose(i + parity, parity)

            @block.scalar
            def _(act):
                with pairs(act, 0, SAMPLES) as i:
                    for parity in range(2):
                        b = i + parity
                        act.wait_ge(turned_ready, b + 1)
                        nc.scalar.activation(s.norm_hi[:, bass.ds(b, 1), :], turned[parity][:, 0:TOKENS], ACT.Copy,
                                             accum_out=s.pooled[:, bass.ds(b, 1)]).then_inc(high_ready, 1)


def route(nc, s, stage):
    with ExitStack() as ctx:
        sb, ps, sem = sb_maker(nc, ctx), ps_maker(nc, ctx), sem_maker(nc, ctx, stage)
        hidden = sb(stage + "_hidden", [ROUTER_H, SAMPLES], F32)
        logits = sb(stage + "_logits", [SAMPLES, ZONES], F32)
        probs = sb(stage + "_probs", [SAMPLES, ZONES], F32)
        best = sb(stage + "_best", [SAMPLES, 8], F32)
        best_at = sb(stage + "_best_at", [SAMPLES, 8], U32)
        column = sb(stage + "_column", [SAMPLES, 4], F32)
        zone_number = sb(stage + "_zone_number", [SAMPLES, TOP_K], F32)
        weights = sb(stage + "_weights", [SAMPLES, TOP_K, P], F32)
        hidden_ps = ps(stage + "_hidden_ps", [ROUTER_H, SAMPLES])
        logits_ps = ps(stage + "_logits_ps", [SAMPLES, ZONES])
        spread = ps(stage + "_spread", [P, UNITS])
        numbers = ps(stage + "_numbers", [1, UNITS])
        hidden_in, hidden_ready, logits_ready, max_ready, exp_ready, chosen, spread_ready, links = (
            sem(n) for n in ("hidden_in", "hidden_ready", "logits_ready", "max_ready", "exp_ready", "chosen",
                             "spread_ready", "links"))
        MAX, SUM, TOP_SUM, INVERSE = range(4)

        with nc.Block() as block:
            @block.tensor
            def _(pe):
                nc.tensor.matmul(hidden_ps[:, :], s.router_w1[:, :], s.pooled[:, :],
                                 start=True, stop=True).then_inc(hidden_in, 1)
                pe.wait_ge(hidden_ready, 1)
                nc.tensor.matmul(logits_ps[:, :], hidden[:, :], s.router_w2[:, :], start=True, stop=False)
                nc.tensor.matmul(logits_ps[:, :], s.ones_row[:, 0:SAMPLES], s.router_b2[:, :],
                                 start=False, stop=True).then_inc(logits_ready, 1)
                pe.wait_ge(chosen, 1)
                for k in range(TOP_K):
                    to = slice(k * SAMPLES, (k + 1) * SAMPLES)
                    nc.tensor.matmul(spread[:, to], weights[:, k, :], s.ident32[0:SAMPLES, 0:SAMPLES],
                                     start=True, stop=True)
                    last = nc.tensor.matmul(numbers[:, to], zone_number[:, k:k + 1],
                                            s.ident32[0:SAMPLES, 0:SAMPLES], start=True, stop=True)
                last.then_inc(spread_ready, 1)

            @block.scalar
            def _(act):
                act.wait_ge(hidden_in, 1)
                nc.scalar.activation(hidden[:, :], hidden_ps[:, :], ACT.Tanh, bias=s.router_b1[:, :],
                                     scale=1.0 / TOKENS).then_inc(hidden_ready, 1)
                act.wait_ge(max_ready, 1)
                nc.scalar.activation(probs[:, :], logits[:, :], ACT.Exp, bias=column[:, MAX:MAX + 1],
                                     accum_out=column[:, SUM:SUM + 1]).then_inc(exp_ready, 1)

            @block.vector
            def _(dve):
                link = Chain(dve, links)
                dve.wait_ge(logits_ready, 1)
                link(nc.vector.tensor_copy(logits[:, :], logits_ps[:, :]))
                nc.vector.tensor_reduce(column[:, MAX:MAX + 1], logits[:, :], AX.X, ALU.max,
                                        negate=True).then_inc(max_ready, 1)
                dve.wait_ge(exp_ready, 1)
                link(nc.vector.reciprocal(column[:, INVERSE:INVERSE + 1], column[:, SUM:SUM + 1]))
                link(nc.vector.tensor_scalar(probs[:, :], probs[:, :], column[:, INVERSE:INVERSE + 1], None, ALU.mult))
                link(nc.vector.max(best[:, :], probs[:, :]))
                link(nc.vector.max_index(best_at[:, :], best[:, :], probs[:, :]))
                link(nc.vector.reduce_sum(column[:, TOP_SUM:TOP_SUM + 1], best[:, 0:TOP_K], AX.X))
                link(nc.vector.reciprocal(column[:, INVERSE:INVERSE + 1], column[:, TOP_SUM:TOP_SUM + 1]))
                nc.vector.tensor_copy(zone_number[:, :], best_at[:, 0:TOP_K])
                nc.vector.tensor_scalar(weights[:, :, :], best[:, 0:TOP_K].unsqueeze(2).to_broadcast([SAMPLES, TOP_K, P]),
                                        column[:, INVERSE:INVERSE + 1], None, ALU.mult).then_inc(chosen, 1)
                dve.wait_ge(spread_ready, 1)
                nc.vector.tensor_copy(s.unit_zone[:, :], numbers[:, :])
                nc.vector.tensor_scalar(s.unit_scale[:, :], spread[:, :], s.hidden_scale[:, :], None, ALU.mult)


def zones(nc, s, stage):
    with ExitStack() as ctx:
        sb, ps, sem = sb_maker(nc, ctx), ps_maker(nc, ctx), sem_maker(nc, ctx, stage)
        hidden = [sb(f"{stage}_hidden{i}", [P, CHUNKS, TOKENS], F32) for i in range(2)]
        hid_hi = [sb(f"{stage}_hid_hi{i}", [P, CHUNKS, TOKENS], F16) for i in range(2)]
        hid_lo = [sb(f"{stage}_hid_lo{i}", [P, CHUNKS, TOKENS], F16) for i in range(2)]
        result = [sb(f"{stage}_result{i}", [P, TOKENS], F32) for i in range(2)]
        hidden_ps = [ps(f"{stage}_hidden_ps{i}", [P, CHUNKS, TOKENS]) for i in range(2)]
        result_ps = [ps(f"{stage}_result_ps{i}", [P, 512]) for i in range(2)]
        turned = ps(stage + "_turned", [P, 512])
        first, gelu_done, split, high, second, copied, turned_ready, added = (
            sem(n) for n in ("first", "gelu_done", "split", "high", "second", "copied", "turned_ready", "added"))

        with nc.Block() as block:
            @block.tensor
            def _(pe):
                def zone_of(b, k):
                    return pe.value_load(s.unit_zone[0:1, bass.ds(b + k * SAMPLES, 1)], min_val=0,
                                         max_val=ZONES - 1)

                def first_product(u, b, k, buf):
                    zone = zone_of(b, k)
                    wait(pe, gelu_done, u - 1)
                    x_hi, x_lo = s.norm_hi[:, bass.ds(b, 1), :], s.norm_lo[:, bass.ds(b, 1), :]
                    for c in range(CHUNKS):
                        at = bass.ds(zone * ZONE_HIDDEN + c * P, P)
                        out = hidden_ps[buf][:, c, :]
                        nc.tensor.matmul(out, s.wa_hi[:, at], x_hi, start=True, stop=False)
                        nc.tensor.matmul(out, s.wa_hi[:, at], x_lo, start=False, stop=False)
                        last = nc.tensor.matmul(out, s.wa_lo[:, at], x_hi, start=False, stop=True)
                    last.then_inc(first, 1)

                def second_product(u, b, buf, k, parity, zone):
                    pe.wait_ge(split, u + 1)
                    if k == 0:
                        wait(pe, copied, b - 1)
                    out = result_ps[parity][:, 0:TOKENS]
                    for c in range(CHUNKS):
                        at = bass.ds(zone * ZONE_HIDDEN + c * P, P)
                        hi, lo = hid_hi[buf][:, c, :], hid_lo[buf][:, c, :]
                        nc.tensor.matmul(out, s.wb_hi[:, at], hi, start=(k == 0 and c == 0), stop=False)
                        nc.tensor.matmul(out, s.wb_hi[:, at], lo, start=False, stop=False)
                        last = nc.tensor.matmul(out, s.wb_lo[:, at], hi, start=False,
                                                stop=(k == TOP_K - 1 and c == CHUNKS - 1))
                    last.then_inc(second, 1)

                def turn_back(b, parity):
                    pe.wait_ge(copied, b + 1)
                    wait(pe, added, b)
                    for t in range(TILES):
                        last = nc.tensor.transpose(turned[:, t * P:(t + 1) * P],
                                                   result[parity][:, t * P:(t + 1) * P], s.ident32[:, :])
                    last.then_inc(turned_ready, 1)

                def sample(b, parity, is_first=False, is_last=False):
                    for k in range(TOP_K):
                        u = TOP_K * b + k
                        zone = zone_of(b, k)
                        if not (is_last and k == TOP_K - 1):
                            to = (b, k + 1) if k < TOP_K - 1 else (b + 1, 0)
                            first_product(u + 1, *to, (parity + k + 1) % 2)
                        second_product(u, b, (parity + k) % 2, k, parity, zone)
                        if k == 0 and not is_first:
                            turn_back(b - 1, 1 - parity)

                first_product(0, 0, 0, 0)
                sample(0, 0, is_first=True)
                with pairs(pe, 1, SAMPLES - 1) as i:
                    sample(i, 1)
                    sample(i + 1, 0)
                sample(SAMPLES - 1, 1, is_last=True)
                turn_back(SAMPLES - 1, 1)

            @block.scalar
            def _(act):
                def gelu(u, buf):
                    act.wait_ge(first, u + 1)
                    wait(act, split, u - 1)
                    nc.scalar.activation(hidden[buf][:, :, :], hidden_ps[buf][:, :, :], ACT.Gelu_apprx_tanh,
                                         scale=s.gelu_scale[:, :]).then_inc(gelu_done, 1)

                def copy_result(b, parity):
                    act.wait_ge(second, TOP_K * (b + 1))
                    wait(act, turned_ready, b - 1)
                    nc.scalar.activation(result[parity][:, :], result_ps[parity][:, 0:TOKENS], ACT.Copy,
                                         scale=s.zone_out_scale[:, :]).then_inc(copied, 1)

                def sample(b, parity, is_first=False):
                    for k in range(TOP_K):
                        gelu(TOP_K * b + k, (parity + k) % 2)
                        if k == 0 and not is_first:
                            copy_result(b - 1, 1 - parity)

                sample(0, 0, is_first=True)
                sample(1, 1)
                with pairs(act, 2, SAMPLES) as i:
                    sample(i, 0)
                    sample(i + 1, 1)
                copy_result(SAMPLES - 1, 1)

            @block.vector
            def _(dve):
                def split_unit(u, b, k, buf):
                    dve.wait_ge(gelu_done, u + 1)
                    wait(dve, second, u - 1)
                    scale = s.unit_scale[:, bass.ds(b + k * SAMPLES, 1)]
                    nc.vector.tensor_scalar(hid_hi[buf][:, :, :], hidden[buf][:, :, :], scale, None,
                                            ALU.mult).then_inc(high, 1)
                    dve.wait_ge(high, u + 1)
                    nc.vector.scalar_tensor_tensor(hid_lo[buf][:, :, :], hidden[buf][:, :, :], scale,
                                                   hid_hi[buf][:, :, :], ALU.mult, ALU.subtract).then_inc(split, 1)

                def add(b):
                    dve.wait_ge(turned_ready, b + 1)
                    rows = tile_of(s.x_res, b)
                    nc.vector.tensor_tensor(rows, rows, turned[:, 0:TOKENS].rearrange("p (t d) -> p t d", t=TILES),
                                            ALU.add).then_inc(added, 1)

                def sample(b, parity, is_first=False):
                    for k in range(TOP_K):
                        split_unit(TOP_K * b + k, b, k, (parity + k) % 2)
                        if k == 1 and not is_first:
                            add(b - 1)

                sample(0, 0, is_first=True)
                with pairs(dve, 1, SAMPLES - 1) as i:
                    sample(i, 1)
                    sample(i + 1, 0)
                sample(SAMPLES - 1, 1)
                add(SAMPLES - 1)


def splat_attention(nc, s, stage):
    with ExitStack() as ctx:
        sb, ps, sem = sb_maker(nc, ctx), ps_maker(nc, ctx), sem_maker(nc, ctx, stage)
        norm = RowNorm(nc, s, ctx, stage, 1)
        normed, norm_ready = norm.out[0], norm.ready
        normed_t = sb(stage + "_normed_t", [P, TOKENS], F32)
        masks = [sb(f"{stage}_lin{i}", [P, 2, TOKENS], F32) for i in range(2)]
        with_square = [sb(f"{stage}_with_square{i}", [P, 2, TOKENS], F32) for i in range(2)]
        features = [sb(f"{stage}_features{i}", [P, FTILES, TOKENS], F32) for i in range(2)]
        q_low = sb(stage + "_q_low", [P, FTILES, TOKENS], F16)
        k_high = sb(stage + "_k_high", [P, FTILES, TOKENS], F16)
        q1, q2, k1, k2 = ([sb(f"{stage}_{n}_{i}", [P, FTILES, TOKENS], F16) for i in range(2)]
                          for n in ("q1", "q2", "k1", "k2"))
        probs = [sb(f"{stage}_probs{i}", [P, TILES, 2, TOKENS], F32) for i in range(2)]
        inverse = sb(stage + "_inverse", [P, TILES * HEADS], F32)
        mixed = sb(stage + "_mixed", [P, TILES * HEADS, HEAD_DIM], F32)
        mixed_t = sb(stage + "_mixed_t", [P, TOKENS], F32)
        logits_ps = [ps(f"{stage}_logits_ps{i}", [P, TILES, 2, TOKENS]) for i in range(2)]
        mixed_ps = ps(stage + "_mixed_ps", [P, 512])
        work_ps = [ps(f"{stage}_work_ps{i}", [P, 2, TOKENS]) for i in range(2)]
        turn_ps = ps(stage + "_turn_ps", [P, 512])
        mixed_out = mixed_ps[:, 0:TILES * HEADS * (HEAD_DIM + 1)].rearrange("p (n c) -> p n c", c=HEAD_DIM + 1)
        (normt_ps, normt_ready, proj_ready, v_ready, masks_ready, squares_ready, values_ready,
         feat_ps, feat_ready, parts_ready, fill_ready, fill_done, negmax_ps, shift_ready, logits_ready, exp_done,
         pv_done, mixed_ready, mixedt_ps, mixedt_ready, out_ready, added, link_parts, link_out) = (
            sem(n) for n in (
                "normt_ps", "normt_ready", "proj_ready", "v_ready", "masks_ready", "squares_ready",
                "values_ready", "feat_ps", "feat_ready", "parts_ready", "fill_ready", "fill_done", "negmax_ps",
                "shift_ready", "logits_ready", "exp_done", "pv_done", "mixed_ready", "mixedt_ps", "mixedt_ready",
                "out_ready", "added", "link_parts", "link_out"))

        def heads_of(u):
            return u % HEAD_GROUPS, (2 * (u // HEAD_GROUPS), 2 * (u // HEAD_GROUPS) + 1)

        FILLS = MAX_FILLS // (HEAD_UNITS // 2)

        with nc.Block() as block:
            @block.tensor
            def _(pe):
                def transpose_norm(b):
                    pe.wait_ge(norm_ready, b + 1)
                    wait(pe, added, b - 1)
                    for t in range(TILES):
                        last = nc.tensor.transpose(turn_ps[:, t * P:(t + 1) * P], normed[:, t, :], s.ident32[:, :])
                    last.then_inc(normt_ps, 1)

                def project(b):
                    pe.wait_ge(normt_ready, b + 1)
                    for t in range(TILES):
                        last = nc.tensor.matmul(turn_ps[:, t * P:(t + 1) * P], normed_t[:, t * P:(t + 1) * P],
                                                s.wv[:, :], start=True, stop=True)
                    last.then_inc(v_ready, 1)
                    wait(pe, fill_done, MAX_FILLS * b)
                    for k, w in enumerate((s.wq_pairs, s.wk_pairs)):
                        for pair in range(2):
                            last = nc.tensor.matmul(work_ps[k][:, pair, :],
                                                    w[:, 2 * pair:2 * pair + 2, :, :].rearrange("d t r c -> d (t r c)"),
                                                    normed_t[:, :], start=True, stop=True)
                        last.then_inc(proj_ready, 1)

                def feature_product(b, k):
                    pe.wait_ge(squares_ready, 2 * b + 2)
                    wait(pe, feat_ready, 2 * b + k)
                    for pair in range(2):
                        for half in range(2):
                            rows = slice(2 * GROUP * half, 2 * GROUP * (half + 1))
                            last = nc.tensor.matmul(work_ps[half][:, pair, :], s.feature_w[rows, pair, :],
                                                    with_square[k][rows, pair, :], start=True, stop=True)
                    last.then_inc(feat_ps, 1)

                def max_fill(b, parity, f):
                    tile, (group, tiles) = f // HEAD_UNITS, heads_of(f % HEAD_UNITS)
                    rows = slice(GROUP * group, GROUP * (group + 1))
                    if f == 0:
                        pe.wait_ge(parts_ready, 2 * b + 2)
                    if f >= 2:
                        pe.wait_ge(fill_done, MAX_FILLS * b + f - 1)
                    for n, t in enumerate(tiles):
                        last = nc.tensor.matmul(work_ps[f % 2][:, n, :], q1[parity][rows, t, tile * P:(tile + 1) * P],
                                                k1[parity][rows, t, :], start=True, stop=True)
                    last.then_inc(fill_ready, 1)

                def transpose_negmax(b, tile):
                    pe.wait_ge(fill_done, MAX_FILLS * (b + 1))
                    if tile == 0:
                        pe.wait_ge(values_ready, b + 1)
                    else:
                        pe.wait_ge(shift_ready, TILES * b + tile)
                    for t in range(FTILES):
                        last = nc.tensor.matmul(turn_ps[:, t * P:(t + 1) * P], s.neg_max[:, tile, t, :],
                                                s.ident16[:, :], start=True, stop=True)
                    last.then_inc(negmax_ps, 1)

                def logits(b, parity, u):
                    n = HEAD_UNITS * b + u
                    if u == 0:
                        pe.wait_ge(shift_ready, TILES * (b + 1))
                    wait(pe, exp_done, n - 1)
                    group, tiles = heads_of(u)
                    rows = slice(GROUP * group, GROUP * (group + 1))
                    for key_tile in range(TILES):
                        keys = slice(key_tile * P, (key_tile + 1) * P)
                        for h, t in enumerate(tiles):
                            out = logits_ps[u % 2][:, key_tile, h, :]
                            nc.tensor.matmul(out, k1[parity][rows, t, keys], q1[parity][rows, t, :],
                                             start=True, stop=False)
                            last = nc.tensor.matmul(out, k2[parity][rows, t, keys], q2[parity][rows, t, :],
                                                    start=False, stop=True)
                    last.then_inc(logits_ready, 1)

                def mix(b, parity, u):
                    pe.wait_ge(exp_done, HEAD_UNITS * b + u + 1)
                    if u == 0:
                        wait(pe, mixed_ready, b)
                    group, tiles = heads_of(u)
                    for h, t in enumerate(tiles):
                        head = HEAD_GROUPS * t + group
                        for tile in range(TILES):
                            for key_tile in range(TILES):
                                last = nc.tensor.matmul(
                                    mixed_out[:, tile * HEADS + head, :],
                                    probs[u % 2][:, key_tile, h, tile * P:(tile + 1) * P],
                                    s.values[:, parity, key_tile, head, :],
                                    start=(key_tile == 0), stop=(key_tile == TILES - 1))
                    last.then_inc(pv_done, 1)

                def output(b):
                    pe.wait_ge(mixed_ready, b + 1)
                    for t in range(TILES):
                        last = nc.tensor.transpose(turn_ps[:, t * P:(t + 1) * P],
                                                   mixed[:, t * HEADS:(t + 1) * HEADS, :].rearrange("p h c -> p (h c)"),
                                                   s.ident32[:, :])
                    last.then_inc(mixedt_ps, 1)
                    pe.wait_ge(mixedt_ready, b + 1)
                    for t in range(TILES):
                        last = nc.tensor.matmul(turn_ps[:, t * P:(t + 1) * P], mixed_t[:, t * P:(t + 1) * P],
                                                s.wo[:, :], start=True, stop=True)
                    last.then_inc(out_ready, 1)

                def prepare(b, parity, u):
                    if u == 0:
                        transpose_norm(b)
                    elif u == 1:
                        project(b)
                    elif u in (2, 3):
                        feature_product(b, u - 2)
                    else:
                        for f in range(FILLS * (u - 4), FILLS * (u - 3)):
                            max_fill(b, parity, f)
                    if u == HEAD_UNITS - 1:
                        transpose_negmax(b, 0)
                        transpose_negmax(b, 1)
                        logits(b, parity, 0)

                def slot(b, parity, is_last=False):
                    for u in range(HEAD_UNITS):
                        if u < HEAD_UNITS - 1:
                            logits(b, parity, u + 1)
                        if not is_last and u < HEAD_UNITS - 1:
                            mix(b, parity, u)
                            prepare(b + 1, 1 - parity, u)
                        elif not is_last:
                            prepare(b + 1, 1 - parity, u)
                            mix(b, parity, u)
                        else:
                            mix(b, parity, u)
                    output(b)

                for u in range(HEAD_UNITS):
                    prepare(0, 0, u)
                slot(0, 0)
                with pairs(pe, 1, SAMPLES - 1) as i:
                    slot(i, 1)
                    slot(i + 1, 0)
                slot(SAMPLES - 1, 1, is_last=True)

            @block.scalar
            def _(act):
                def exps(b, u):
                    n = HEAD_UNITS * b + u
                    act.wait_ge(logits_ready, n + 1)
                    wait(act, pv_done, n - 1)
                    nc.scalar.activation(probs[u % 2][:, :, :, :], logits_ps[u % 2][:, :, :, :],
                                         ACT.Exp).then_inc(exp_done, 1)

                def prepare(b, u):
                    if u == 0:
                        act.wait_ge(normt_ps, b + 1)
                        wait(act, proj_ready, 2 * b)
                        nc.scalar.activation(normed_t[:, :], turn_ps[:, 0:TOKENS], ACT.Copy).then_inc(normt_ready, 1)
                    elif u == 1:
                        for k in range(2):
                            act.wait_ge(proj_ready, 2 * b + k + 1)
                            wait(act, squares_ready, 2 * b + k - 1)
                            nc.scalar.activation(masks[k][:, :, :], work_ps[k][:, :, :], ACT.Identity,
                                                 bias=s.linear_rows[:, :],
                                                 scale=s.square_rows[:, :]).then_inc(masks_ready, 1)
                    elif u in (2, 3):
                        k = u - 2
                        act.wait_ge(feat_ps, 2 * b + k + 1)
                        wait(act, parts_ready, 2 * b + k - 1)
                        for t in range(FTILES):
                            last = nc.scalar.activation(features[k][:, t, :], work_ps[t % 2][:, t // 2, :], ACT.Exp,
                                                        bias=s.feature_bias[:, k * FTILES + t:k * FTILES + t + 1])
                        last.then_inc(feat_ready, 1)

                def slot(b, is_last=False):
                    for u in range(HEAD_UNITS):
                        exps(b, u)
                        if not is_last:
                            prepare(b + 1, u)
                    act.wait_ge(mixedt_ps, b + 1)
                    nc.scalar.activation(mixed_t[:, :], turn_ps[:, 0:TOKENS], ACT.Copy).then_inc(mixedt_ready, 1)

                for u in range(HEAD_UNITS):
                    prepare(0, u)
                slot(0)
                with act.Fori(1, SAMPLES - 1, 1) as i:
                    slot(i)
                slot(SAMPLES - 1, is_last=True)

            @block.vector
            def _(dve):
                def prepare(b, parity, u):
                    if u == 0:
                        wait(dve, normt_ps, b)
                        norm.apply(dve, b, parity, normed)
                    elif u == 1:
                        if not (isinstance(b, int) and b + 1 >= SAMPLES):
                            norm.statistics(dve, b + 1, 1 - parity)
                        dve.wait_ge(v_ready, b + 1)
                        nc.vector.tensor_copy(s.values[:, parity, :, :, 0:HEAD_DIM],
                                              turn_ps[:, 0:TOKENS].rearrange("p (t h c) -> p t h c", t=TILES, h=HEADS)
                                              ).then_inc(values_ready, 1)
                        for k in range(2):
                            dve.wait_ge(masks_ready, 2 * b + k + 1)
                            wait(dve, feat_ps, 2 * b + k - 1)
                            nc.vector.tensor_tensor(with_square[k][:, :, :], masks[k][:, :, :], work_ps[k][:, :, :],
                                                    ALU.mult).then_inc(squares_ready, 1)
                    elif u == 2:
                        link = Chain(dve, link_parts, 2 * b)
                        dve.wait_ge(feat_ready, 2 * b + 1)
                        link(nc.vector.tensor_copy(q1[parity][:, :, :], features[0][:, :, :]))
                        nc.vector.tensor_tensor(q_low[:, :, :], features[0][:, :, :], q1[parity][:, :, :],
                                                ALU.subtract).then_inc(parts_ready, 1)
                    elif u == 3:
                        link = Chain(dve, link_parts, 2 * b + 1)
                        dve.wait_ge(feat_ready, 2 * b + 2)
                        link(nc.vector.tensor_copy(k_high[:, :, :], features[1][:, :, :]))
                        nc.vector.tensor_scalar(k2[parity][:, :, :], k_high[:, :, :], s.first_copy[:, :],
                                                s.shift_row[:, :], ALU.mult, ALU.add)
                        nc.vector.scalar_tensor_tensor(k1[parity][:, :, :], k_high[:, :, :], s.minus_second[:, :],
                                                       features[1][:, :, :], ALU.mult, ALU.add).then_inc(parts_ready, 1)
                    else:
                        for f in range(FILLS * (u - 4), FILLS * (u - 3)):
                            tile, (group, tiles) = f // HEAD_UNITS, heads_of(f % HEAD_UNITS)
                            dve.wait_ge(fill_ready, MAX_FILLS * b + f + 1)
                            if f % HEAD_UNITS == 0:
                                wait(dve, negmax_ps, TILES * b + tile - 1)
                            nc.vector.tensor_reduce(
                                s.neg_max[:, tile, tiles[0]:tiles[1] + 1, GROUP * group + SPLATS],
                                work_ps[f % 2][:, :, :], AX.X, ALU.max, negate=True).then_inc(fill_done, 1)
                    if u == HEAD_UNITS - 1:
                        for tile in range(TILES):
                            dve.wait_ge(negmax_ps, TILES * b + tile + 1)
                            at = slice(tile * P, (tile + 1) * P)
                            nc.vector.scalar_tensor_tensor(
                                q2[parity][:, :, at], q_low[:, :, at], s.first_copy[:, :],
                                turn_ps[:, :].rearrange("p (t i) -> p t i", t=FTILES),
                                ALU.mult, ALU.add).then_inc(shift_ready, 1)

                def slot(b, parity, is_last=False):
                    for u in range(HEAD_UNITS):
                        if not is_last:
                            prepare(b + 1, 1 - parity, u)
                    dve.wait_ge(pv_done, HEAD_UNITS * (b + 1))
                    link = Chain(dve, link_out, b)
                    link(nc.vector.reciprocal(inverse[:, :], mixed_out[:, :, HEAD_DIM]))
                    nc.vector.tensor_tensor(mixed[:, :, :], mixed_out[:, :, 0:HEAD_DIM],
                                            inverse[:, :].unsqueeze(2).to_broadcast([P, TILES * HEADS, HEAD_DIM]),
                                            ALU.mult).then_inc(mixed_ready, 1)
                    dve.wait_ge(out_ready, b + 1)
                    rows = tile_of(s.x_res, b)
                    nc.vector.tensor_tensor(rows, rows, turn_ps[:, 0:TOKENS].rearrange("p (t d) -> p t d", t=TILES),
                                            ALU.add).then_inc(added, 1)

                norm.statistics(dve, 0, 0)
                for u in range(HEAD_UNITS):
                    prepare(0, 0, u)
                slot(0, 0)
                with pairs(dve, 1, SAMPLES - 3) as i:
                    slot(i, 1)
                    slot(i + 1, 0)
                slot(SAMPLES - 3, 1)
                slot(SAMPLES - 2, 0)
                slot(SAMPLES - 1, 1, is_last=True)

            @block.gpsimd
            def _(pool):
                norm.powers(pool)


def splines(nc, s, stage, out=None):
    with ExitStack() as ctx:
        sb, ps, sem = sb_maker(nc, ctx), ps_maker(nc, ctx), sem_maker(nc, ctx, stage)
        norm = RowNorm(nc, s, ctx, stage, 2)
        normed, norm_ready = norm.out, norm.ready
        normed_t = [sb(f"{stage}_normed_t{i}", [P, TOKENS], F32) for i in range(2)]
        bent = [sb(f"{stage}_bent{i}", [P, HALF_KNOTS, TOKENS], F32) for i in range(2)]
        turned = [ps(f"{stage}_turned{i}", [P, 512]) for i in range(2)]
        inner = [ps(f"{stage}_inner{i}", [P, 512]) for i in range(2)]
        result = [ps(f"{stage}_result{i}", [P, 512]) for i in range(2)]
        (turned_ready, normt_ready, inner_ready, bent_ready, result_ready, biased, added, stored) = (sem(n) for n in ("turned_ready", "normt_ready", "inner_ready", "bent_ready",
                                    "result_ready", "biased", "added", "stored"))

        with nc.Block() as block:
            @block.vector
            def _(dve):
                def apply(b, parity):
                    wait(dve, turned_ready, b - 1)
                    norm.apply(dve, b, parity, normed[parity])

                def add(b, parity):
                    dve.wait_ge(result_ready, b + 1)
                    dve.wait_ge(biased, b + 1)
                    rows = tile_of(s.x_res, b)
                    nc.vector.tensor_tensor(rows, rows,
                                            result[parity][:, 0:TOKENS].rearrange("p (t d) -> p t d", t=TILES),
                                            ALU.add).then_inc(added, 1)

                norm.statistics(dve, 0, 0)
                norm.statistics(dve, 1, 1)
                apply(0, 0)
                apply(1, 1)
                norm.statistics(dve, 2, 0)
                apply(2, 0)
                norm.statistics(dve, 3, 1)
                add(0, 0)
                with pairs(dve, 1, SAMPLES - 3) as i:
                    for step, parity in ((0, 1), (1, 0)):
                        apply(i + step + 2, parity)
                        norm.statistics(dve, i + step + 3, 1 - parity)
                        add(i + step, parity)
                apply(SAMPLES - 1, 1)
                for b in range(SAMPLES - 3, SAMPLES):
                    add(b, b % 2)

            @block.gpsimd
            def _(pool):
                def bias(b):
                    wait(pool, norm_ready, b + 1)
                    rows = tile_of(s.x_res, b)
                    nc.gpsimd.tensor_tensor(rows, rows, s.half_bias[:, :, :], ALU.add).then_inc(biased, 1)

                norm.powers(pool, after=bias)

            @block.tensor
            def _(pe):
                def prepare(b, parity):
                    pe.wait_ge(norm_ready, b + 1)
                    wait(pe, normt_ready, b - 1)
                    for t in range(TILES):
                        last = nc.tensor.transpose(turned[parity][:, t * P:(t + 1) * P],
                                                   normed[parity][:, t, :], s.ident32[:, :])
                    last.then_inc(turned_ready, 1)

                def enter(b, parity):
                    pe.wait_ge(normt_ready, b + 1)
                    wait(pe, bent_ready, b - 1)
                    nc.tensor.matmul(inner[parity][:, 0:TOKENS], s.win2[:, :], normed_t[parity][:, :],
                                     start=True, stop=True).then_inc(inner_ready, 1)

                def leave(b, parity):
                    pe.wait_ge(bent_ready, b + 1)
                    wait(pe, added, b - 1)
                    for t in range(TILES):
                        for k in range(HALF_KNOTS):
                            last = nc.tensor.matmul(result[parity][:, t * P:(t + 1) * P],
                                                    bent[parity][:, k, t * P:(t + 1) * P], s.knot_out[:, k, :],
                                                    start=(k == 0), stop=(k == HALF_KNOTS - 1))
                    last.then_inc(result_ready, 1)

                prepare(0, 0)
                prepare(1, 1)
                enter(0, 0)
                prepare(2, 0)
                enter(1, 1)
                leave(0, 0)
                with pairs(pe, 1, SAMPLES - 3) as i:
                    for step, parity in ((0, 1), (1, 0)):
                        prepare(i + step + 2, parity)
                        enter(i + step + 1, 1 - parity)
                        leave(i + step, parity)
                prepare(SAMPLES - 1, 1)
                enter(SAMPLES - 2, 0)
                leave(SAMPLES - 3, 1)
                enter(SAMPLES - 1, 1)
                leave(SAMPLES - 2, 0)
                leave(SAMPLES - 1, 1)

            @block.scalar
            def _(act):
                def copy(b, parity):
                    act.wait_ge(turned_ready, b + 1)
                    wait(act, inner_ready, b - 1)
                    nc.scalar.activation(normed_t[parity][:, :], turned[parity][:, 0:TOKENS],
                                         ACT.Copy).then_inc(normt_ready, 1)

                def bend(b, parity):
                    act.wait_ge(inner_ready, b + 1)
                    wait(act, result_ready, b - 1)
                    for k in range(HALF_KNOTS):
                        last = nc.scalar.activation(bent[parity][:, k, :], inner[parity][:, 0:TOKENS], ACT.Relu,
                                                    bias=s.relu_bias[:, k:k + 1], scale=s.relu_scale[:, k:k + 1])
                    last.then_inc(bent_ready, 1)

                copy(0, 0)
                copy(1, 1)
                bend(0, 0)
                with pairs(act, 1, SAMPLES - 1) as i:
                    for step, parity in ((0, 1), (1, 0)):
                        copy(i + step + 1, 1 - parity)
                        bend(i + step, parity)
                bend(SAMPLES - 1, 1)

            if out is not None:
                @block.sync
                def _(sp):
                    rows = out.rearrange("b (t p) d -> p (b t) d", p=P)
                    with sp.Fori(0, SAMPLES, 1) as b:
                        sp.wait_ge(added, b + 1)
                        sp.dma_start(rows[:, bass.ds(b * TILES, TILES), :], tile_of(s.x_res, b)).then_inc(stored, 16)
                    sp.wait_ge(stored, 16 * SAMPLES)


def causal_attention(nc, s, stage):
    BLOCKS = ((0, 0), (1, 0), (1, 1))
    with ExitStack() as ctx:
        sb, ps, sem = sb_maker(nc, ctx), ps_maker(nc, ctx), sem_maker(nc, ctx, stage)
        norm = RowNorm(nc, s, ctx, stage, 1)
        normed, norm_ready = norm.out[0], norm.ready
        normed_t = sb(stage + "_normed_t", [P, TOKENS], F32)
        qk = [sb(f"{stage}_qk{i}", [P, 2, TOKENS], F32) for i in range(2)]
        v = [sb(f"{stage}_v{i}", [P, TILES, P], F32) for i in range(2)]
        masked = sb(stage + "_masked", [P, 3 * P], F32)
        neg_max = sb(stage + "_neg_max", [P, TILES], F32)
        probs = [sb(f"{stage}_probs{i}", [P, 3 * P], F32) for i in range(2)]
        sums = [sb(f"{stage}_sums{i}", [P, TILES], F32) for i in range(2)]
        inverse = [sb(f"{stage}_inverse{i}", [P, TILES], F32) for i in range(2)]
        probs_t = sb(stage + "_probs_t", [P, 3 * P], F32)
        turn_ps = ps(stage + "_turn_ps", [P, 512])
        qk_ps = ps(stage + "_qk_ps", [P, 2, TOKENS])
        v_ps = ps(stage + "_v_ps", [P, 512])
        scores_ps = ps(stage + "_scores_ps", [P, 512])
        probst_ps = ps(stage + "_probst_ps", [P, 512])
        result_ps = ps(stage + "_result_ps", [P, 512])
        (turned, normt_ready, qk_done, v_done, qk_ready, v_ready, scores_done, masked_ready, max_ready,
         exp_done, probst_done, probst_ready, result_done, added, link_sum) = (
            sem(n) for n in ("turned", "normt_ready", "qk_done", "v_done", "qk_ready", "v_ready",
                             "scores_done", "masked_ready", "max_ready", "exp_done", "probst_done", "probst_ready",
                             "result_done", "added", "link_sum"))
        SCALE = 1.0 / math.sqrt(P)
        SPANS = (slice(0, P), slice(P, 3 * P))

        with nc.Block() as block:
            def run(engine, *steps):
                def turn(b, parity):
                    for step, lead in steps:
                        if not isinstance(b, int) or 0 <= b + lead < SAMPLES:
                            step(b + lead, (parity + lead) % 2)

                for b in range(-2, 2):
                    turn(b, b % 2)
                with pairs(engine, 2, SAMPLES - 4) as i:
                    turn(i, 0)
                    turn(i + 1, 1)
                for b in range(SAMPLES - 4, SAMPLES):
                    turn(b, b % 2)

            @block.vector
            def _(dve):
                def projections(b, parity):
                    wait(dve, turned, b)
                    norm.apply(dve, b, parity, normed)
                    if not (isinstance(b, int) and b + 1 >= SAMPLES):
                        norm.statistics(dve, b + 1, 1 - parity)

                def values(b, parity):
                    dve.wait_ge(v_done, b + 1)
                    wait(dve, result_done, b - 1)
                    nc.vector.tensor_tensor(v[parity][:, :, :], v_ps[:, 0:TOKENS].rearrange("p (t c) -> p t c", t=TILES),
                                            s.attn1_bv[:, :].unsqueeze(1).to_broadcast([P, TILES, P]),
                                            ALU.add).then_inc(v_ready, 1)

                def scores(b, parity):
                    dve.wait_ge(scores_done, b + 1)
                    wait(dve, exp_done, b)
                    nc.vector.scalar_tensor_tensor(masked[:, :], scores_ps[:, 0:3 * P], SCALE, s.causal[:, :],
                                                   ALU.mult, ALU.add).then_inc(masked_ready, 1)
                    dve.wait_ge(masked_ready, b + 1)
                    for t in range(TILES):
                        last = nc.vector.tensor_reduce(neg_max[:, t:t + 1], masked[:, SPANS[t]], AX.X, ALU.max,
                                                       negate=True)
                    last.then_inc(max_ready, 1)

                def result(b, parity):
                    link = Chain(dve, link_sum, b)
                    dve.wait_ge(exp_done, b + 1)
                    link(nc.vector.reciprocal(inverse[parity][:, :], sums[parity][:, :]))
                    dve.wait_ge(result_done, b + 1)
                    for t in range(TILES):
                        rows = tile_of(s.x_res, b, t)
                        last = nc.vector.scalar_tensor_tensor(rows, result_ps[:, t * P:(t + 1) * P],
                                                              inverse[parity][:, t:t + 1], rows, ALU.mult, ALU.add)
                    last.then_inc(added, 1)

                norm.statistics(dve, 0, 0)
                run(dve, (projections, 2), (result, 0), (values, 2), (scores, 1))

            @block.gpsimd
            def _(pool):
                norm.powers(pool)

            @block.tensor
            def _(pe):
                def projections(b, parity):
                    pe.wait_ge(norm_ready, b + 1)
                    wait(pe, normt_ready, b)
                    for t in range(TILES):
                        last = nc.tensor.transpose(turn_ps[:, t * P:(t + 1) * P], normed[:, t, :], s.ident32[:, :])
                    last.then_inc(turned, 1)
                    pe.wait_ge(normt_ready, b + 1)
                    wait(pe, v_ready, b)
                    for t in range(TILES):
                        last = nc.tensor.matmul(v_ps[:, t * P:(t + 1) * P], normed_t[:, t * P:(t + 1) * P],
                                                s.attn1_w[:, 2 * P:3 * P], start=True, stop=True)
                    last.then_inc(v_done, 1)
                    wait(pe, qk_ready, b)
                    for k in range(2):
                        last = nc.tensor.matmul(qk_ps[:, k, :], s.attn1_w[:, k * P:(k + 1) * P], normed_t[:, :],
                                                start=True, stop=True)
                    last.then_inc(qk_done, 1)

                def scores(b, parity):
                    pe.wait_ge(qk_ready, b + 1)
                    wait(pe, masked_ready, b)
                    for t in range(TILES):
                        last = nc.tensor.matmul(scores_ps[:, SPANS[t]], qk[parity][:, 0, t * P:(t + 1) * P],
                                                qk[parity][:, 1, 0:(t + 1) * P], start=True, stop=True)
                    last.then_inc(scores_done, 1)

                def turn_probs(b, parity):
                    pe.wait_ge(exp_done, b + 1)
                    wait(pe, probst_ready, b)
                    for n in range(len(BLOCKS)):
                        last = nc.tensor.transpose(probst_ps[:, n * P:(n + 1) * P],
                                                   probs[parity][:, n * P:(n + 1) * P], s.ident32[:, :])
                    last.then_inc(probst_done, 1)

                def result(b, parity):
                    pe.wait_ge(probst_ready, b + 1)
                    pe.wait_ge(v_ready, b + 1)
                    wait(pe, added, b)
                    for n, (tile, key_tile) in enumerate(BLOCKS):
                        last = nc.tensor.matmul(result_ps[:, tile * P:(tile + 1) * P], probs_t[:, n * P:(n + 1) * P],
                                                v[parity][:, key_tile, :], start=(key_tile == 0),
                                                stop=(key_tile == tile))
                    last.then_inc(result_done, 1)

                run(pe, (turn_probs, 0), (projections, 2), (result, 0), (scores, 1))

            @block.scalar
            def _(act):
                def projections(b, parity):
                    act.wait_ge(turned, b + 1)
                    wait(act, qk_done, b)
                    nc.scalar.activation(normed_t[:, :], turn_ps[:, 0:TOKENS], ACT.Copy).then_inc(normt_ready, 1)
                    act.wait_ge(qk_done, b + 1)
                    wait(act, scores_done, b - 1)
                    for k in range(2):
                        last = nc.scalar.activation(qk[parity][:, k, :], qk_ps[:, k, :], ACT.Identity,
                                                    bias=s.attn1_bqk[:, k:k + 1])
                    last.then_inc(qk_ready, 1)

                def scores(b, parity):
                    act.wait_ge(max_ready, b + 1)
                    wait(act, probst_done, b - 1)
                    for t in range(TILES):
                        last = nc.scalar.activation(probs[parity][:, SPANS[t]], masked[:, SPANS[t]], ACT.Exp,
                                                    bias=neg_max[:, t:t + 1], accum_out=sums[parity][:, t:t + 1])
                    last.then_inc(exp_done, 1)

                def result(b, parity):
                    act.wait_ge(probst_done, b + 1)
                    wait(act, result_done, b)
                    nc.scalar.activation(probs_t[:, :], probst_ps[:, 0:3 * P], ACT.Copy).then_inc(probst_ready, 1)

                run(act, (result, 0), (projections, 2), (scores, 1))


def build(nc, a, out):
    with ExitStack() as ctx:
        sb = sb_maker(nc, ctx)
        s = Store()
        s.x_res = sb("x_res", [P, SAMPLES * TILES, P], F32)
        s.norm_hi = sb("norm_hi", [P, SAMPLES, TOKENS], F16)
        s.norm_lo = sb("norm_lo", [P, SAMPLES, TOKENS], F16)
        s.pooled = sb("pooled", [P, SAMPLES], F32)
        s.ident32 = sb("ident32", [P, P], F32)
        s.ident16 = sb("ident16", [P, P], F16)
        s.causal = sb("causal", [P, 3 * P], F32)
        s.row_index = sb("row_index", [P, 1], I32)
        s.ones_row = sb("ones_row", [1, P], F32)
        s.eps = sb("eps", [P, TILES], F32)
        s.minus_half = sb("minus_half", [P, TILES], F32)
        s.wa_hi, s.wa_lo, s.wb_hi, s.wb_lo = (
            sb(name, [P, ZONES * ZONE_HIDDEN], F16) for name in ("wa_hi", "wa_lo", "wb_hi", "wb_lo"))
        s.router_w1 = sb("router_w1", [P, ROUTER_H], F32)
        s.router_w2 = sb("router_w2", [ROUTER_H, ZONES], F32)
        s.router_b1 = sb("router_b1", [ROUTER_H, 1], F32)
        s.router_b2 = sb("router_b2", [1, ZONES], F32)
        s.unit_zone = sb("unit_zone", [1, UNITS], U32)
        s.unit_scale = sb("unit_scale", [P, UNITS], F32)
        s.gelu_scale = sb("gelu_scale", [P, 1], F32)
        s.hidden_scale = sb("hidden_scale", [P, 1], F32)
        s.zone_out_scale = sb("zone_out_scale", [P, 1], F32)
        s.wq_pairs = sb("wq_pairs", [P, FTILES, 2, GROUP], F32)
        s.wk_pairs = sb("wk_pairs", [P, FTILES, 2, GROUP], F32)
        s.wv = sb("wv", [P, P], F32)
        s.wo = sb("wo", [P, P], F32)
        s.feature_w = sb("feature_w", [P, 2, P], F32)
        s.feature_bias = sb("feature_bias", [P, 2 * FTILES], F32)
        s.first_copy = sb("first_copy", [P, 1], F32)
        s.minus_second = sb("minus_second", [P, 1], F32)
        s.shift_row = sb("shift_row", [P, 1], F32)
        s.linear_rows = sb("linear_rows", [P, 1], F32)
        s.square_rows = sb("square_rows", [P, 1], F32)
        s.neg_max = sb("neg_max", [P, TILES, FTILES, P], F16)
        s.values = sb("values", [P, 2, TILES, HEADS, HEAD_DIM + 1], F32)
        s.attn1_w = sb("attn1_w", [P, 3 * P], F32)
        s.attn1_bqk = sb("attn1_bqk", [P, 2], F32)
        s.attn1_bv = sb("attn1_bv", [P, P], F32)
        s.win2 = sb("win2", [P, P], F32)
        s.relu_scale = sb("relu_scale", [P, HALF_KNOTS], F32)
        s.relu_bias = sb("relu_bias", [P, HALF_KNOTS], F32)
        s.knot_out = sb("knot_out", [P, HALF_KNOTS, P], F32)
        s.half_bias = sb("half_bias", [P, TILES, P], F32)

        with ExitStack() as setup:
            st = sb_maker(nc, setup)
            s.stage_a = st("stage_a", [P, ZONES * ZONE_HIDDEN], F32)
            s.stage_b = st("stage_b", [P, ZONES * ZONE_HIDDEN], F32)
            s.qkv_rows = st("qkv_rows", [P, 3, P], F32)
            s.out_rows = st("out_rows", [P, P], F32)
            s.centers = st("centers", [P, SPLATS], F32)
            s.deltas = st("deltas", [P, SPLATS], F32)
            s.log_scales = st("log_scales", [P, SPLATS], F32)
            s.log_amps = st("log_amps", [P, SPLATS], F32)
            s.movement = st("movement", [P, 1], F32)
            s.temperature = st("temperature", [P, 1], F32)
            s.bin2 = st("bin2", [P, 1], F32)
            s.knot_b1 = st("knot_b1", [P, HALF_KNOTS], F32)
            s.knot_w2 = st("knot_w2", [P, HALF_KNOTS], F32)
            s.wout2 = st("wout2", [P, P], F32)
            s.b2_col = st("b2_col", [SPLINES, 1], F32)
            s.bout_row = st("bout_row", [1, P], F32)
            load_and_constants(nc, s, a)
            prepare_zones(nc, s)
            prepare_splats(nc, s)
            prepare_splines(nc, s)

        zone_norm(nc, s, "norm_a")
        route(nc, s, "route_a")
        zones(nc, s, "zones_a")
        splat_attention(nc, s, "splat")
        zone_norm(nc, s, "norm_b")
        route(nc, s, "route_b")
        zones(nc, s, "zones_b")
        splines(nc, s, "spline_a")
        causal_attention(nc, s, "causal")
        splines(nc, s, "spline_b", out)


INPUTS = ["L0_attn_x", "L0_attn_splat_centers", "L0_attn_splat_deltas", "L0_attn_splat_log_scales",
          "L0_attn_splat_log_amplitudes", "L0_attn_movement_scale", "L0_attn_temperature", "L0_attn_qkv_w",
          "L0_attn_out_w", "L0_ffn_W1", "L0_ffn_b1", "L0_ffn_W2", "L0_ffn_b2", "L0_ffn_Wa", "L0_ffn_Wb",
          "L1_attn_W", "L1_attn_b", "L1_ffn_Win", "L1_ffn_bin_", "L1_ffn_W1", "L1_ffn_b1", "L1_ffn_W2",
          "L1_ffn_b2", "L1_ffn_Wout", "L1_ffn_bout"]


def kernel(**inputs):
    import numpy as np
    import concourse.bacc as bacc
    from concourse.bass_utils import run_bass_kernel_spmd

    nc = bacc.Bacc("TRN2", target_bir_lowering=False, num_devices=1)
    arrays, aps = {}, {}
    for name in INPUTS:
        array = np.ascontiguousarray(inputs[name])
        if array.ndim == 0:
            array = array.reshape(1)
        arrays[name] = array
        aps[name] = nc.dram_tensor(name, array.shape, mybir.dt.from_np(array.dtype), kind="ExternalInput").ap()
    out = nc.dram_tensor("out", (SAMPLES, TOKENS, P), F32, kind="ExternalOutput").ap()
    build(nc, aps, out)
    results = run_bass_kernel_spmd(nc, [arrays], core_ids=[0])
    return results.results[0]["out"]
```

```python
import math
from contextlib import ExitStack

import concourse.bass as bass
from concourse import mybir

F32 = mybir.dt.float32
F16 = mybir.dt.float16
BF16 = mybir.dt.bfloat16
I32 = mybir.dt.int32
U32 = mybir.dt.uint32
ALU = mybir.AluOpType
ACT = mybir.ActivationFunctionType
AX = mybir.AxisListType

P = 128
SAMPLES = 32
TOKENS = 256
TILES = TOKENS // P
EPS = 1e-5

ZONES, ZONE_HIDDEN, TOP_K, ROUTER_H = 8, 512, 3, 32
CHUNKS = ZONE_HIDDEN // P
UNITS = SAMPLES * TOP_K
WEIGHT_SHIFT = 2.0 ** 8
HIDDEN_SHIFT = 2.0 ** 6

HEADS, SPLATS, HEAD_DIM = 16, 16, 8
GROUP = 32
HEAD_GROUPS = P // GROUP
FTILES = HEADS // HEAD_GROUPS
HEAD_UNITS = HEADS // 2
VALUE_PARTS = 3
SUM_COLUMN = VALUE_PARTS * HEAD_DIM
PROB_BUFFERS = 4
PROB_SHIFT = 5.0
MAX_FILLS = TILES * HEAD_UNITS

SPLINES, KNOTS = 64, 16
HALF_KNOTS = KNOTS // 2
MASKED = -9000000000000000.0


def wait(engine, semaphore, value):
    if isinstance(value, int) and value <= 0:
        return
    engine.wait_ge(semaphore, value)


def pairs(engine, first, end):
    return engine.Fori(first, end - 1, 2)


class Chain:

    def __init__(self, engine, semaphore, base=0):
        self.engine, self.semaphore, self.base, self.n = engine, semaphore, base, 0

    def __call__(self, instruction):
        self.n += 1
        instruction.then_inc(self.semaphore, 1)
        self.engine.wait_ge(self.semaphore, self.base + self.n)


def tile_of(x_res, sample, tile=None):
    if isinstance(sample, int):
        rows = x_res[:, TILES * sample:TILES * (sample + 1), :]
    else:
        rows = x_res[:, bass.ds(sample * TILES, TILES), :]
    return rows if tile is None else rows[:, tile, :]


class RowNorm:

    def __init__(self, nc, s, ctx, stage, buffers):
        sb, sem = sb_maker(nc, ctx), sem_maker(nc, ctx, stage)
        self.nc, self.s = nc, s
        self.stats = sb(stage + "_stats", [P, TILES, 6], F32)
        self.moments = [sb(f"{stage}_moments{i}", [P, TILES, 2], F32) for i in range(2)]
        self.shifted = sb(stage + "_shifted", [P, TILES], F32)
        self.rstd = [sb(f"{stage}_rstd{i}", [P, TILES], F32) for i in range(2)]
        self.out = [sb(f"{stage}_normed{i}", [P, TILES, P], F32) for i in range(buffers)]
        self.stats_ready, self.moments_ready, self.shifted_ready, self.rstd_ready, self.ready = (
            sem(n) for n in ("stats_ready", "moments_ready", "shifted_ready", "rstd_ready", "norm_ready"))

    def statistics(self, dve, b, parity):
        wait(dve, self.moments_ready, b)
        for t in range(TILES):
            last = self.nc.vector.bn_stats(self.stats[:, t, :], tile_of(self.s.x_res, b, t))
        last.then_inc(self.stats_ready, 1)
        value = b + 1 if isinstance(b, int) else dve.to_reg(b + 1)
        dve.wait_ge(self.stats_ready, 1)
        dve.wait_ge(self.stats_ready, value)
        for t in range(TILES):
            last = self.nc.vector.bn_aggr(self.moments[parity][:, t, :], self.stats[:, t, :])
        last.then_inc(self.moments_ready, 1)

    def power(self, pool, b, parity):
        pool.wait_ge(self.moments_ready, b + 1)
        wait(pool, self.rstd_ready, b)
        self.nc.gpsimd.tensor_tensor(self.shifted[:, :], self.moments[parity][:, :, 1], self.s.eps[:, :],
                                     ALU.add).then_inc(self.shifted_ready, 1)
        pool.wait_ge(self.shifted_ready, b + 1)
        wait(pool, self.ready, b - 1)
        self.nc.gpsimd.tensor_tensor(self.rstd[parity][:, :], self.shifted[:, :], self.s.minus_half[:, :],
                                     ALU.pow).then_inc(self.rstd_ready, 1)

    def powers(self, pool, after=None):
        def power(b, parity):
            self.power(pool, b, parity)

        power(0, 0)
        power(1, 1)
        if after is not None:
            after(0)
        with pairs(pool, 2, SAMPLES) as i:
            for parity in range(2):
                power(i + parity, parity)
                if after is not None:
                    after(i + parity - 1)
        if after is not None:
            after(SAMPLES - 1)

    def apply(self, dve, b, parity, out):
        dve.wait_ge(self.rstd_ready, b + 1)
        for t in range(TILES):
            last = self.nc.vector.tensor_scalar(out[:, t, :], tile_of(self.s.x_res, b, t),
                                                self.moments[parity][:, t, 0:1], self.rstd[parity][:, t:t + 1],
                                                ALU.subtract, ALU.mult)
        last.then_inc(self.ready, 1)


class Store:
    pass


def sb_maker(nc, ctx):
    return lambda name, shape, dt: ctx.enter_context(nc.sbuf_tensor(name, shape, dt))


def ps_maker(nc, ctx):
    return lambda name, shape: ctx.enter_context(nc.psum_tensor(name, shape, F32))


def sem_maker(nc, ctx, stage):
    return lambda name: ctx.enter_context(nc.semaphore(f"{stage}_{name}"))


def load_and_constants(nc, s, a):
    with ExitStack() as ctx:
        sem = sem_maker(nc, ctx, "load")
        loads = []

        def load(dst, src):
            loads.append((dst, src))

        load(s.stage_a[:, :].rearrange("d (e f) -> d e f", e=ZONES), a["L0_ffn_Wa"].rearrange("e d f -> d e f"))
        load(s.stage_b[:, :].rearrange("f (e c d) -> f e c d", e=ZONES, c=CHUNKS),
             a["L0_ffn_Wb"].rearrange("e (c f) d -> f e c d", f=P))
        load(s.qkv_rows[:, :, :], a["L0_attn_qkv_w"].rearrange("(k o) d -> o k d", o=P))
        load(s.out_rows[:, :], a["L0_attn_out_w"])
        load(s.router_w1[:, :], a["L0_ffn_W1"])
        load(s.router_w2[:, :], a["L0_ffn_W2"])
        load(s.router_b1[:, :], a["L0_ffn_b1"].unsqueeze(1))
        load(s.router_b2[:, :], a["L0_ffn_b2"].unsqueeze(0))
        for h in range(HEADS):
            rows = slice(h * HEAD_DIM, (h + 1) * HEAD_DIM)
            load(s.centers[rows, :], a["L0_attn_splat_centers"][h].rearrange("s d -> d s"))
            load(s.deltas[rows, :], a["L0_attn_splat_deltas"][h].rearrange("s d -> d s"))
            load(s.log_scales[rows, :], a["L0_attn_splat_log_scales"][h].partition_broadcast(HEAD_DIM))
            load(s.log_amps[rows, :], a["L0_attn_splat_log_amplitudes"][h].partition_broadcast(HEAD_DIM))
        load(s.movement[:, :], a["L0_attn_movement_scale"].partition_broadcast(P).unsqueeze(1))
        load(s.temperature[:, :], a["L0_attn_temperature"].partition_broadcast(P).unsqueeze(1))
        load(s.attn1_w[:, :], a["L1_attn_W"])
        bias = a["L1_attn_b"]
        for k in range(2):
            load(s.attn1_bqk[:, k:k + 1], bias[k * P:(k + 1) * P].unsqueeze(1))
        load(s.attn1_bv[:, :], bias[2 * P:3 * P].partition_broadcast(P))
        for c in range(2):
            half = slice(c * SPLINES, (c + 1) * SPLINES)
            knots = slice(c * HALF_KNOTS, (c + 1) * HALF_KNOTS)
            load(s.win2[:, half], a["L1_ffn_Win"])
            load(s.bin2[half, :], a["L1_ffn_bin_"].unsqueeze(1))
            load(s.relu_scale[half, :], a["L1_ffn_W1"][:, knots])
            load(s.knot_b1[half, :], a["L1_ffn_b1"][:, knots])
            load(s.knot_w2[half, :], a["L1_ffn_W2"][:, knots])
            load(s.wout2[half, :], a["L1_ffn_Wout"])
        load(s.b2_col[:, :], a["L1_ffn_b2"].unsqueeze(1))
        load(s.bout_row[:, :], a["L1_ffn_bout"].unsqueeze(0))
        loaded = sem("loaded")
        loaded_by_pool = sem("loaded_by_pool")
        zeroed = sem("zeroed")

        with nc.Block() as block:
            @block.sync
            def _(sp):
                for dst, src in loads[:2]:
                    sp.dma_start(dst, src, allow_slow_non_contiguous=True).then_inc(loaded, 16)
                sp.dma_start(s.x_res[:, :, :],
                             a["L0_attn_x"].rearrange("b (t p) d -> p (b t) d", p=P)).then_inc(s.x_loaded, 16)
                for dst, src in loads[2::3]:
                    sp.dma_start(dst, src, allow_slow_non_contiguous=True).then_inc(loaded, 16)
                sp.wait_ge(loaded, 16 * (len(loads) - len(loads[4::3])))
                sp.wait_ge(loaded_by_pool, 16 * len(loads[4::3]))

            @block.scalar
            def _(act):
                for dst, src in loads[3::3]:
                    act.dma_start(dst, src, allow_slow_non_contiguous=True).then_inc(loaded, 16)

            @block.gpsimd
            def _(pool):
                for dst, src in loads[4::3]:
                    pool.dma_start(dst, src, allow_slow_non_contiguous=True).then_inc(loaded_by_pool, 16)
                nc.gpsimd.memset(s.ident32[:, :], 0.0)
                nc.gpsimd.memset(s.ident16[:, :], 0.0)
                nc.gpsimd.memset(s.causal[:, :], 0.0).then_inc(zeroed, 1)
                pool.wait_ge(zeroed, 1)
                for m in (s.ident32, s.ident16):
                    nc.gpsimd.affine_select(out=m[:, :], in_=m[:, :], compare_op=ALU.not_equal, fill=1.0,
                                            base=0, pattern=[[-1, P]], channel_multiplier=1)
                for c in (0, 2):
                    part = s.causal[:, c * P:(c + 1) * P]
                    nc.gpsimd.affine_select(out=part, in_=part, compare_op=ALU.is_ge, fill=MASKED,
                                            base=0, pattern=[[-1, P]], channel_multiplier=1)
                nc.gpsimd.iota(s.row_index[:, :], pattern=[[0, 1]], base=0, channel_multiplier=1)

            @block.vector
            def _(dve):
                nc.vector.memset(s.ones_row[:, :], 1.0)
                nc.vector.memset(s.eps[:, :], EPS)
                nc.vector.memset(s.minus_half[:, :], -0.5)
                nc.vector.memset(s.neg_max[:, :, :, :], 0.0)
                nc.vector.memset(s.values[:, :, :, :, 0:SUM_COLUMN + 1], 1.0)
                nc.vector.memset(s.values[:, :, :, :, SUM_COLUMN + 1:GROUP], 0.0)
                nc.vector.memset(s.prob_shift[:, :], PROB_SHIFT)


def prepare_zones(nc, s):
    with ExitStack() as ctx:
        sb, ps, sem = sb_maker(nc, ctx), ps_maker(nc, ctx), sem_maker(nc, ctx, "zonew")
        row_max = sb("zonew_row_max", [P, 2], F32)
        all_max = sb("zonew_all_max", [1, 2], F32)
        power = sb("zonew_power", [1, 2], F32)
        powers = sb("zonew_powers", [P, 2], F32)
        inverse = sb("zonew_inverse", [P, 2], F32)
        scale = sb("zonew_scale", [P, 2], F32)
        spread = ps("zonew_spread", [P, 512])
        maxima, turned, power_ready, spread_ready, links = (
            sem(n) for n in ("maxima", "turned", "power_ready", "spread_ready", "links"))

        with nc.Block() as block:
            @block.vector
            def _(dve):
                link = Chain(dve, links)
                for k, w in enumerate((s.stage_a, s.stage_b)):
                    last = nc.vector.tensor_reduce(row_max[:, k:k + 1], w[:, :], AX.X, ALU.max,
                                                   apply_absolute_value=True)
                last.then_inc(maxima, 1)
                dve.wait_ge(turned, 1)
                link(nc.vector.tensor_reduce(all_max[:, :], spread[0:1, 0:2 * P].rearrange("a (k p) -> a k p", k=2),
                                             AX.X, ALU.max))
                link(nc.vector.tensor_scalar_max(all_max[:, :], all_max[:, :], 1e-30))
                nc.vector.tensor_scalar(power[:, :].bitcast(I32), all_max[:, :].bitcast(I32), 0x7F800000, None,
                                        ALU.bitwise_and).then_inc(power_ready, 1)
                dve.wait_ge(spread_ready, 1)
                link(nc.vector.tensor_copy(powers[:, :], spread[:, 0:2]))
                link(nc.vector.reciprocal(inverse[:, :], powers[:, :]))
                link(nc.vector.tensor_scalar_mul(scale[:, :], inverse[:, :], WEIGHT_SHIFT))
                nc.vector.tensor_scalar_mul(s.gelu_scale[:, :], powers[:, 0:1], 1.0 / WEIGHT_SHIFT)
                nc.vector.tensor_scalar_mul(s.hidden_scale[:, :], inverse[:, 0:1], HIDDEN_SHIFT)
                nc.vector.scalar_tensor_tensor(s.zone_out_scale[:, :], powers[:, 0:1],
                                               0.5 / (HIDDEN_SHIFT * WEIGHT_SHIFT), powers[:, 1:2],
                                               ALU.mult, ALU.mult)
                for k, (w, hi, lo) in enumerate(((s.stage_a, s.wa_hi, s.wa_lo), (s.stage_b, s.wb_hi, s.wb_lo))):
                    link(nc.vector.tensor_scalar(hi[:, :], w[:, :], scale[:, k:k + 1], None, ALU.mult))
                    nc.vector.scalar_tensor_tensor(lo[:, :], w[:, :], scale[:, k:k + 1], hi[:, :],
                                                   ALU.mult, ALU.subtract)

            @block.tensor
            def _(pe):
                pe.wait_ge(maxima, 1)
                for k in range(2):
                    last = nc.tensor.matmul(spread[0:1, k * P:(k + 1) * P], row_max[:, k:k + 1], s.ident32[:, :],
                                            start=True, stop=True)
                last.then_inc(turned, 1)
                pe.wait_ge(power_ready, 1)
                nc.tensor.matmul(spread[:, 0:2], s.ones_row[:, :], power[:, :],
                                 start=True, stop=True).then_inc(spread_ready, 1)


def prepare_splats(nc, s):
    with ExitStack() as ctx:
        sb, ps, sem = sb_maker(nc, ctx), ps_maker(nc, ctx), sem_maker(nc, ctx, "splatw")
        bits = sb("splatw_bits", [P, 4], I32)
        index = sb("splatw_index", [P, 4], F32)
        in_group = sb("splatw_in_group", [P, HEAD_GROUPS], F32)
        in_tile = sb("splatw_in_tile", [P, FTILES], F32)
        sig = sb("splatw_sig", [P, 1], F32)
        log_temp = sb("splatw_log_temp", [P, 1], F32)
        temp = sb("splatw_temp", [P, 1], F32)
        c = sb("splatw_c", [P, SPLATS], F32)
        var = sb("splatw_var", [P, SPLATS], F32)
        scales = sb("splatw_scales", [P, SPLATS], F32)
        small = sb("splatw_small", [P, 4, SPLATS], F32)
        wide = sb("splatw_wide", [P, 4, HEAD_GROUPS, 2, SPLATS], F32)
        turned = ps("splatw_turned", [P, 4 * P])
        consts = ps("splatw_consts", [P, 2 * FTILES])
        (transposed, act_done, temp_ready, links, wide_ready, consts_ready, moved) = (
            sem(n) for n in ("transposed", "act_done", "temp_ready", "links", "wide_ready", "consts_ready", "moved"))
        LINEAR, SQUARE, KEY_CONST, QUERY_CONST = range(4)

        with nc.Block() as block:
            @block.tensor
            def _(pe):
                for k in range(3):
                    nc.tensor.transpose(turned[:, k * P:(k + 1) * P], s.qkv_rows[:, k, :], s.ident32[:, :])
                nc.tensor.transpose(turned[:, 3 * P:4 * P], s.out_rows[:, :], s.ident32[:, :]).then_inc(transposed, 1)
                pe.wait_ge(wide_ready, 1)
                for k, kind in enumerate((QUERY_CONST, KEY_CONST)):
                    last = nc.tensor.matmul(consts[:, k * FTILES:(k + 1) * FTILES],
                                            wide[:, kind, :, :, :].rearrange("p g r s -> p (g r s)"),
                                            in_tile[:, :], start=True, stop=True)
                last.then_inc(consts_ready, 1)

            @block.scalar
            def _(act):
                nc.scalar.activation(scales[:, :], s.log_scales[:, :], ACT.Exp).then_inc(act_done, 1)
                nc.scalar.activation(sig[:, :], s.movement[:, :], ACT.Sigmoid).then_inc(act_done, 1)
                act.wait_ge(temp_ready, 1)
                nc.scalar.activation(log_temp[:, :], temp[:, :], ACT.Ln).then_inc(act_done, 1)

            @block.vector
            def _(dve):
                link = Chain(dve, links)
                nc.vector.tensor_scalar(temp[:, :], s.temperature[:, :], 0.1, 10.0,
                                        ALU.max, ALU.min).then_inc(temp_ready, 1)
                link(nc.vector.tensor_scalar(bits[:, 0:1], s.row_index[:, :], 3, 3,
                                             ALU.arith_shift_right, ALU.bitwise_and))
                link(nc.vector.tensor_scalar(bits[:, 1:2], s.row_index[:, :], 5, 3,
                                             ALU.arith_shift_right, ALU.bitwise_and))
                link(nc.vector.tensor_scalar(bits[:, 2:3], s.row_index[:, :], GROUP - 1, None, ALU.bitwise_and))
                link(nc.vector.tensor_scalar(bits[:, 3:4], s.row_index[:, :], 2 * GROUP - 1, None, ALU.bitwise_and))
                link(nc.vector.tensor_copy(index[:, :], bits[:, :]))
                for g in range(HEAD_GROUPS):
                    nc.vector.tensor_scalar(in_group[:, g:g + 1], index[:, 0:1], float(g), None, ALU.is_equal)
                    nc.vector.tensor_scalar(in_tile[:, g:g + 1], index[:, 1:2], float(g), None, ALU.is_equal)
                nc.vector.tensor_scalar(s.first_copy[:, :], index[:, 2:3], float(SPLATS), None, ALU.is_lt)
                nc.vector.tensor_scalar(s.minus_second[:, :], index[:, 2:3], float(SPLATS), -1.0, ALU.is_ge, ALU.mult)
                nc.vector.tensor_scalar(s.shift_row[:, :], index[:, 2:3], float(SPLATS), None, ALU.is_equal)
                nc.vector.tensor_scalar(s.linear_rows[:, :], index[:, 3:4], float(GROUP), None, ALU.is_lt)
                link(nc.vector.tensor_scalar(s.square_rows[:, :], index[:, 3:4], float(GROUP), None, ALU.is_ge))
                dve.wait_ge(act_done, 2)
                link(nc.vector.tensor_scalar(c[:, :], s.deltas[:, :], sig[:, :], 0.2, ALU.mult, ALU.mult))
                link(nc.vector.tensor_tensor(c[:, :], c[:, :], s.centers[:, :], ALU.add))
                link(nc.vector.tensor_scalar(scales[:, :], scales[:, :], 0.01, 2.0, ALU.max, ALU.min))
                link(nc.vector.tensor_tensor(var[:, :], scales[:, :], scales[:, :], ALU.mult))
                link(nc.vector.tensor_scalar_add(var[:, :], var[:, :], 1e-8))
                link(nc.vector.reciprocal(var[:, :], var[:, :]))
                link(nc.vector.tensor_scalar_mul(small[:, SQUARE, :], var[:, :], -0.5))
                link(nc.vector.scalar_tensor_tensor(small[:, LINEAR, :], c[:, :], -2.0, small[:, SQUARE, :],
                                                    ALU.mult, ALU.mult))
                link(nc.vector.scalar_tensor_tensor(small[:, KEY_CONST, :], small[:, LINEAR, :], -0.5, c[:, :],
                                                    ALU.mult, ALU.mult))
                dve.wait_ge(act_done, 3)
                link(nc.vector.tensor_scalar(scales[:, :], s.log_amps[:, :], math.log(1e-6), math.log(10.0),
                                             ALU.max, ALU.min))
                link(nc.vector.tensor_scalar(scales[:, :], scales[:, :], log_temp[:, :], 1.0 / HEAD_DIM,
                                             ALU.subtract, ALU.mult))
                link(nc.vector.tensor_tensor(small[:, QUERY_CONST, :], scales[:, :], small[:, KEY_CONST, :], ALU.add))
                for g in range(HEAD_GROUPS):
                    for copy in range(2):
                        last = nc.vector.tensor_scalar(wide[:, :, g, copy, :], small[:, :, :], in_group[:, g:g + 1],
                                                       None, ALU.mult)
                last.then_inc(wide_ready, 1)
                dve.wait_ge(transposed, 1)
                for k, w in enumerate((s.wq_pairs, s.wk_pairs)):
                    src = turned[:, k * P:(k + 1) * P].rearrange("d (t c) -> d t c", t=FTILES)
                    for copy in range(2):
                        nc.vector.tensor_copy(w[:, :, copy, :], src)
                nc.vector.tensor_copy(s.wv[:, :], turned[:, 2 * P:3 * P])
                nc.vector.tensor_copy(s.wo[:, :], turned[:, 3 * P:4 * P])
                dve.wait_ge(consts_ready, 1)
                nc.vector.tensor_copy(s.feature_bias[:, :], consts[:, :])

            @block.sync
            def _(sp):
                sp.wait_ge(wide_ready, 1)
                n = 0
                for t in range(FTILES):
                    rows = slice(t * GROUP, (t + 1) * GROUP)
                    for k, kind in enumerate((LINEAR, SQUARE)):
                        to = 2 * GROUP * (t % 2) + GROUP * k
                        sp.dma_start(s.feature_w[to:to + GROUP, t // 2, :],
                                     wide[rows, kind, :, :, :].rearrange("p g r s -> p (g r s)")).then_inc(moved, 16)
                        n += 16
                sp.wait_ge(moved, n)


def prepare_splines(nc, s):
    with ExitStack() as ctx:
        sb, ps, sem = sb_maker(nc, ctx), ps_maker(nc, ctx), sem_maker(nc, ctx, "splinew")
        scaled = sb("splinew_scaled", [P, HALF_KNOTS], F32)
        half_row = sb("splinew_half_row", [1, P], F32)
        half_b2 = sb("splinew_half_b2", [SPLINES, P], F32)
        out_bias = ps("splinew_out_bias", [P, P])
        links, rows_ready, bias_ready = (sem(n) for n in ("links", "rows_ready", "bias_ready"))

        with nc.Block() as block:
            @block.vector
            def _(dve):
                link = Chain(dve, links)
                link(nc.vector.tensor_scalar(scaled[:, :], s.relu_scale[:, :], s.bin2[:, :], None, ALU.mult))
                nc.vector.tensor_tensor(s.relu_bias[:, :], scaled[:, :], s.knot_b1[:, :], ALU.add)
                for k in range(HALF_KNOTS):
                    nc.vector.tensor_scalar(s.knot_out[:, k, :], s.wout2[:, :], s.knot_w2[:, k:k + 1], 0.5,
                                            ALU.mult, ALU.mult)
                link(nc.vector.memset(half_b2[:, :], 0.5))
                nc.vector.tensor_scalar_mul(half_row[:, :], s.bout_row[:, :], 0.5)
                nc.vector.tensor_scalar(half_b2[:, :], half_b2[:, :], s.b2_col[:, :], None,
                                        ALU.mult).then_inc(rows_ready, 1)
                dve.wait_ge(bias_ready, 1)
                nc.vector.tensor_copy(s.half_bias[:, 0, :], out_bias[:, :])
                nc.vector.tensor_copy(s.half_bias[:, 1, :], out_bias[:, :])

            @block.sync
            def _(sp):
                sp.wait_ge(s.x_loaded, 16)

            @block.tensor
            def _(pe):
                pe.wait_ge(rows_ready, 1)
                nc.tensor.matmul(out_bias[:, :], half_b2[:, :], s.wout2[0:SPLINES, :], start=True, stop=False)
                nc.tensor.matmul(out_bias[:, :], s.ones_row[:, :], half_row[:, :],
                                 start=False, stop=True).then_inc(bias_ready, 1)


def zone_norm(nc, s, stage):
    with ExitStack() as ctx:
        sb, ps, sem = sb_maker(nc, ctx), ps_maker(nc, ctx), sem_maker(nc, ctx, stage)
        norm = RowNorm(nc, s, ctx, stage, 2)
        normed, norm_ready = norm.out, norm.ready
        turned = [ps(f"{stage}_turned{i}", [P, 512]) for i in range(2)]
        turned_ready, high_ready, parts_ready = (
            sem(n) for n in ("turned_ready", "high_ready", "parts_ready"))

        with nc.Block() as block:
            @block.vector
            def _(dve):
                def apply(b, parity):
                    wait(dve, turned_ready, b - 1)
                    norm.apply(dve, b, parity, normed[parity])
                    dve.wait_ge(norm_ready, b + 1)
                    rows = tile_of(s.x_res, b)
                    nc.vector.scalar_tensor_tensor(rows, normed[parity][:, :, :], 0.5, rows, ALU.mult, ALU.add)

                def low(b, parity):
                    dve.wait_ge(high_ready, b + 1)
                    nc.vector.tensor_tensor(s.norm_lo[:, bass.ds(b, 1), :], turned[parity][:, 0:TOKENS],
                                            s.norm_hi[:, bass.ds(b, 1), :], ALU.subtract).then_inc(parts_ready, 1)

                norm.statistics(dve, 0, 0)
                norm.statistics(dve, 1, 1)
                apply(0, 0)
                with pairs(dve, 1, SAMPLES - 1) as i:
                    for step, parity in ((0, 1), (1, 0)):
                        norm.statistics(dve, i + step + 1, 1 - parity)
                        apply(i + step, parity)
                        low(i + step - 1, 1 - parity)
                apply(SAMPLES - 1, 1)
                low(SAMPLES - 2, 0)
                low(SAMPLES - 1, 1)

            @block.gpsimd
            def _(pool):
                norm.powers(pool)

            @block.tensor
            def _(pe):
                def transpose(b, parity):
                    pe.wait_ge(norm_ready, b + 1)
                    wait(pe, parts_ready, b - 1)
                    for t in range(TILES):
                        last = nc.tensor.transpose(turned[parity][:, t * P:(t + 1) * P],
                                                   normed[parity][:, t, :], s.ident32[:, :])
                    last.then_inc(turned_ready, 1)

                transpose(0, 0)
                transpose(1, 1)
                with pairs(pe, 2, SAMPLES) as i:
                    for parity in range(2):
                        transpose(i + parity, parity)

            @block.scalar
            def _(act):
                with pairs(act, 0, SAMPLES) as i:
                    for parity in range(2):
                        b = i + parity
                        act.wait_ge(turned_ready, b + 1)
                        nc.scalar.activation(s.norm_hi[:, bass.ds(b, 1), :], turned[parity][:, 0:TOKENS], ACT.Copy,
                                             accum_out=s.pooled[:, bass.ds(b, 1)]).then_inc(high_ready, 1)


def route(nc, s, stage):
    with ExitStack() as ctx:
        sb, ps, sem = sb_maker(nc, ctx), ps_maker(nc, ctx), sem_maker(nc, ctx, stage)
        hidden = sb(stage + "_hidden", [ROUTER_H, SAMPLES], F32)
        logits = sb(stage + "_logits", [SAMPLES, ZONES], F32)
        probs = sb(stage + "_probs", [SAMPLES, ZONES], F32)
        best = sb(stage + "_best", [SAMPLES, 8], F32)
        best_at = sb(stage + "_best_at", [SAMPLES, 8], U32)
        column = sb(stage + "_column", [SAMPLES, 4], F32)
        zone_number = sb(stage + "_zone_number", [SAMPLES, TOP_K], F32)
        weights = sb(stage + "_weights", [SAMPLES, TOP_K, P], F32)
        number_row = sb(stage + "_number_row", [1, TOP_K, SAMPLES], F32)
        code = sb(stage + "_code", [1, SAMPLES], F32)
        hidden_ps = ps(stage + "_hidden_ps", [ROUTER_H, SAMPLES])
        logits_ps = ps(stage + "_logits_ps", [SAMPLES, ZONES])
        spread = ps(stage + "_spread", [P, UNITS])
        numbers = ps(stage + "_numbers", [1, UNITS])
        hidden_in, hidden_ready, logits_ready, max_ready, exp_ready, chosen, spread_ready, links = (
            sem(n) for n in ("hidden_in", "hidden_ready", "logits_ready", "max_ready", "exp_ready", "chosen",
                             "spread_ready", "links"))
        MAX, SUM, TOP_SUM, INVERSE = range(4)

        with nc.Block() as block:
            @block.tensor
            def _(pe):
                nc.tensor.matmul(hidden_ps[:, :], s.router_w1[:, :], s.pooled[:, :],
                                 start=True, stop=True).then_inc(hidden_in, 1)
                pe.wait_ge(hidden_ready, 1)
                nc.tensor.matmul(logits_ps[:, :], hidden[:, :], s.router_w2[:, :], start=True, stop=False)
                nc.tensor.matmul(logits_ps[:, :], s.ones_row[:, 0:SAMPLES], s.router_b2[:, :],
                                 start=False, stop=True).then_inc(logits_ready, 1)
                pe.wait_ge(chosen, 1)
                for k in range(TOP_K):
                    to = slice(k * SAMPLES, (k + 1) * SAMPLES)
                    nc.tensor.matmul(spread[:, to], weights[:, k, :], s.ident32[0:SAMPLES, 0:SAMPLES],
                                     start=True, stop=True)
                    last = nc.tensor.matmul(numbers[:, to], zone_number[:, k:k + 1],
                                            s.ident32[0:SAMPLES, 0:SAMPLES], start=True, stop=True)
                last.then_inc(spread_ready, 1)

            @block.scalar
            def _(act):
                act.wait_ge(hidden_in, 1)
                nc.scalar.activation(hidden[:, :], hidden_ps[:, :], ACT.Tanh, bias=s.router_b1[:, :],
                                     scale=1.0 / TOKENS).then_inc(hidden_ready, 1)
                act.wait_ge(max_ready, 1)
                nc.scalar.activation(probs[:, :], logits[:, :], ACT.Exp, bias=column[:, MAX:MAX + 1],
                                     accum_out=column[:, SUM:SUM + 1]).then_inc(exp_ready, 1)

            @block.vector
            def _(dve):
                link = Chain(dve, links)
                dve.wait_ge(logits_ready, 1)
                link(nc.vector.tensor_copy(logits[:, :], logits_ps[:, :]))
                nc.vector.tensor_reduce(column[:, MAX:MAX + 1], logits[:, :], AX.X, ALU.max,
                                        negate=True).then_inc(max_ready, 1)
                dve.wait_ge(exp_ready, 1)
                link(nc.vector.reciprocal(column[:, INVERSE:INVERSE + 1], column[:, SUM:SUM + 1]))
                link(nc.vector.tensor_scalar(probs[:, :], probs[:, :], column[:, INVERSE:INVERSE + 1], None, ALU.mult))
                link(nc.vector.max(best[:, :], probs[:, :]))
                link(nc.vector.max_index(best_at[:, :], best[:, :], probs[:, :]))
                link(nc.vector.reduce_sum(column[:, TOP_SUM:TOP_SUM + 1], best[:, 0:TOP_K], AX.X))
                link(nc.vector.reciprocal(column[:, INVERSE:INVERSE + 1], column[:, TOP_SUM:TOP_SUM + 1]))
                nc.vector.tensor_copy(zone_number[:, :], best_at[:, 0:TOP_K])
                nc.vector.tensor_scalar(weights[:, :, :], best[:, 0:TOP_K].unsqueeze(2).to_broadcast([SAMPLES, TOP_K, P]),
                                        column[:, INVERSE:INVERSE + 1], None, ALU.mult).then_inc(chosen, 1)
                dve.wait_ge(spread_ready, 1)
                nc.vector.tensor_scalar(s.unit_scale[:, :], spread[:, :], s.hidden_scale[:, :], None, ALU.mult)
                link(nc.vector.tensor_copy(number_row[:, :, :], numbers[:, :].rearrange("p (k b) -> p k b", k=TOP_K)))
                link(nc.vector.tensor_copy(code[:, :], number_row[:, 0, :]))
                for digit, number, to in ((1, number_row[:, 1, :], SAMPLES), (2, number_row[:, 2, :], SAMPLES),
                                          (TOP_K, number_row[:, 0, 1:SAMPLES], SAMPLES - 1)):
                    link(nc.vector.scalar_tensor_tensor(code[:, 0:to], number, float(ZONES ** digit), code[:, 0:to],
                                                        ALU.mult, ALU.add))
                nc.vector.tensor_copy(s.zone_code[:, :], code[:, :])


def zones(nc, s, stage):
    with ExitStack() as ctx:
        sb, ps, sem = sb_maker(nc, ctx), ps_maker(nc, ctx), sem_maker(nc, ctx, stage)
        hidden = [sb(f"{stage}_hidden{i}", [P, CHUNKS, TOKENS], F32) for i in range(2)]
        hid_hi = [sb(f"{stage}_hid_hi{i}", [P, CHUNKS, TOKENS], F16) for i in range(2)]
        hid_lo = [sb(f"{stage}_hid_lo{i}", [P, CHUNKS, TOKENS], F16) for i in range(2)]
        result = [sb(f"{stage}_result{i}", [P, TOKENS], F32) for i in range(2)]
        hidden_ps = [ps(f"{stage}_hidden_ps{i}", [P, CHUNKS, TOKENS]) for i in range(2)]
        result_ps = [ps(f"{stage}_result_ps{i}", [P, 512]) for i in range(2)]
        turned = ps(stage + "_turned", [P, 512])
        first, gelu_done, split, high, second, copied, turned_ready, added = (
            sem(n) for n in ("first", "gelu_done", "split", "high", "second", "copied", "turned_ready", "added"))

        with nc.Block() as block:
            @block.tensor
            def _(pe):
                def zones_of(b):
                    code = pe.value_load(s.zone_code[0:1, bass.ds(b, 1)], min_val=0,
                                         max_val=ZONES ** (TOP_K + 1) - 1)
                    return [(code // ZONES ** k) % ZONES for k in range(TOP_K + 1)]

                def first_product(u, b, zone, buf):
                    wait(pe, gelu_done, u - 1)
                    x_hi, x_lo = s.norm_hi[:, bass.ds(b, 1), :], s.norm_lo[:, bass.ds(b, 1), :]
                    for c in range(CHUNKS):
                        at = bass.ds(zone * ZONE_HIDDEN + c * P, P)
                        out = hidden_ps[buf][:, c, :]
                        nc.tensor.matmul(out, s.wa_hi[:, at], x_hi, start=True, stop=False)
                        nc.tensor.matmul(out, s.wa_hi[:, at], x_lo, start=False, stop=False)
                        last = nc.tensor.matmul(out, s.wa_lo[:, at], x_hi, start=False, stop=True)
                    last.then_inc(first, 1)

                def second_product(u, b, buf, k, parity, zone):
                    pe.wait_ge(split, u + 1)
                    if k == 0:
                        wait(pe, copied, b - 1)
                    out = result_ps[parity][:, 0:TOKENS]
                    for c in range(CHUNKS):
                        at = bass.ds(zone * ZONE_HIDDEN + c * P, P)
                        hi, lo = hid_hi[buf][:, c, :], hid_lo[buf][:, c, :]
                        nc.tensor.matmul(out, s.wb_hi[:, at], hi, start=(k == 0 and c == 0), stop=False)
                        nc.tensor.matmul(out, s.wb_hi[:, at], lo, start=False, stop=False)
                        last = nc.tensor.matmul(out, s.wb_lo[:, at], hi, start=False,
                                                stop=(k == TOP_K - 1 and c == CHUNKS - 1))
                    last.then_inc(second, 1)

                def turn_back(b, parity):
                    pe.wait_ge(copied, b + 1)
                    wait(pe, added, b)
                    for t in range(TILES):
                        last = nc.tensor.transpose(turned[:, t * P:(t + 1) * P],
                                                   result[parity][:, t * P:(t + 1) * P], s.ident32[:, :])
                    last.then_inc(turned_ready, 1)

                def sample(b, parity, is_first=False, is_last=False):
                    chosen = zones_of(b)
                    for k in range(TOP_K):
                        u = TOP_K * b + k
                        if not (is_last and k == TOP_K - 1):
                            first_product(u + 1, b if k < TOP_K - 1 else b + 1, chosen[k + 1], (parity + k + 1) % 2)
                        second_product(u, b, (parity + k) % 2, k, parity, chosen[k])
                        if k == 0 and not is_first:
                            turn_back(b - 1, 1 - parity)

                first_product(0, 0, zones_of(0)[0], 0)
                sample(0, 0, is_first=True)
                with pairs(pe, 1, SAMPLES - 1) as i:
                    sample(i, 1)
                    sample(i + 1, 0)
                sample(SAMPLES - 1, 1, is_last=True)
                turn_back(SAMPLES - 1, 1)

            @block.scalar
            def _(act):
                def gelu(u, buf):
                    act.wait_ge(first, u + 1)
                    wait(act, split, u - 1)
                    nc.scalar.activation(hidden[buf][:, :, :], hidden_ps[buf][:, :, :], ACT.Gelu_apprx_tanh,
                                         scale=s.gelu_scale[:, :]).then_inc(gelu_done, 1)

                def copy_result(b, parity):
                    act.wait_ge(second, TOP_K * (b + 1))
                    wait(act, turned_ready, b - 1)
                    nc.scalar.activation(result[parity][:, :], result_ps[parity][:, 0:TOKENS], ACT.Copy,
                                         scale=s.zone_out_scale[:, :]).then_inc(copied, 1)

                def sample(b, parity, is_first=False):
                    for k in range(TOP_K):
                        gelu(TOP_K * b + k, (parity + k) % 2)
                        if k == 0 and not is_first:
                            copy_result(b - 1, 1 - parity)

                sample(0, 0, is_first=True)
                sample(1, 1)
                with pairs(act, 2, SAMPLES) as i:
                    sample(i, 0)
                    sample(i + 1, 1)
                copy_result(SAMPLES - 1, 1)

            @block.vector
            def _(dve):
                def split_unit(u, b, k, buf):
                    dve.wait_ge(gelu_done, u + 1)
                    wait(dve, second, u - 1)
                    scale = s.unit_scale[:, bass.ds(b + k * SAMPLES, 1)]
                    nc.vector.tensor_scalar(hid_hi[buf][:, :, :], hidden[buf][:, :, :], scale, None,
                                            ALU.mult).then_inc(high, 1)
                    dve.wait_ge(high, u + 1)
                    nc.vector.scalar_tensor_tensor(hid_lo[buf][:, :, :], hidden[buf][:, :, :], scale,
                                                   hid_hi[buf][:, :, :], ALU.mult, ALU.subtract).then_inc(split, 1)

                def add(b):
                    dve.wait_ge(turned_ready, b + 1)
                    rows = tile_of(s.x_res, b)
                    nc.vector.tensor_tensor(rows, rows, turned[:, 0:TOKENS].rearrange("p (t d) -> p t d", t=TILES),
                                            ALU.add).then_inc(added, 1)

                def sample(b, parity, is_first=False):
                    for k in range(TOP_K):
                        split_unit(TOP_K * b + k, b, k, (parity + k) % 2)
                        if k == 1 and not is_first:
                            add(b - 1)

                sample(0, 0, is_first=True)
                with pairs(dve, 1, SAMPLES - 1) as i:
                    sample(i, 1)
                    sample(i + 1, 0)
                sample(SAMPLES - 1, 1)
                add(SAMPLES - 1)


def splat_attention(nc, s, stage):
    with ExitStack() as ctx:
        sb, ps, sem = sb_maker(nc, ctx), ps_maker(nc, ctx), sem_maker(nc, ctx, stage)
        norm = RowNorm(nc, s, ctx, stage, 1)
        normed, norm_ready = norm.out[0], norm.ready
        normed_t = sb(stage + "_normed_t", [P, TOKENS], F32)
        masks = [sb(f"{stage}_lin{i}", [P, 2, TOKENS], F32) for i in range(2)]
        with_square = [sb(f"{stage}_with_square{i}", [P, 2, TOKENS], F32) for i in range(2)]
        features = [sb(f"{stage}_features{i}", [P, FTILES, TOKENS], F32) for i in range(2)]
        q_low = sb(stage + "_q_low", [P, FTILES, TOKENS], F16)
        k_high = sb(stage + "_k_high", [P, FTILES, TOKENS], F16)
        q1, q2, k1, k2 = ([sb(f"{stage}_{n}_{i}", [P, FTILES, TOKENS], F16) for i in range(2)]
                          for n in ("q1", "q2", "k1", "k2"))
        probs = [sb(f"{stage}_probs{i}", [P, TILES, 2, TOKENS], F32) for i in range(2)]
        probs_hi, probs_lo = ([sb(f"{stage}_{n}_{i}", [P, TILES, 2, TOKENS], F16) for i in range(PROB_BUFFERS)]
                              for n in ("probs_hi", "probs_lo"))
        value_rest = sb(stage + "_value_rest", [P, TILES, HEADS, HEAD_DIM], F32)
        mixed_parts = [sb(f"{stage}_mixed_parts{i}", [P, 2, TOKENS], F32) for i in range(2)]
        summed = sb(stage + "_summed", [P, TILES, HEAD_UNITS, HEAD_DIM], F32)
        inverse = sb(stage + "_inverse", [P, TILES, HEAD_UNITS], F32)
        mixed = sb(stage + "_mixed", [P, TILES, HEADS, HEAD_DIM], F32)
        mixed_t = sb(stage + "_mixed_t", [P, TOKENS], F32)
        logits_ps = [ps(f"{stage}_logits_ps{i}", [P, TILES, 2, TOKENS]) for i in range(2)]
        mixed_ps = ps(stage + "_mixed_ps", [P, 2, TOKENS])
        work_ps = [ps(f"{stage}_work_ps{i}", [P, 2, TOKENS]) for i in range(2)]
        turn_ps = ps(stage + "_turn_ps", [P, 512])
        (normt_ps, normt_ready, proj_ready, v_ready, masks_ready, squares_ready, values_ready,
         feat_ps, feat_ready, parts_ready, fill_ready, fill_done, negmax_ps, shift_ready, logits_ready, exp_done,
         low_ready, pv_done, parts_kept, parts_turned, shared, mixedt_ps, mixedt_ready, out_ready, added, link_parts, link_values,
         link_out) = (
            sem(n) for n in (
                "normt_ps", "normt_ready", "proj_ready", "v_ready", "masks_ready", "squares_ready",
                "values_ready", "feat_ps", "feat_ready", "parts_ready", "fill_ready", "fill_done", "negmax_ps",
                "shift_ready", "logits_ready", "exp_done", "low_ready", "pv_done", "parts_kept", "parts_turned",
                "shared", "mixedt_ps", "mixedt_ready", "out_ready", "added", "link_parts", "link_values", "link_out"))

        def heads_of(u):
            return u % HEAD_GROUPS, (2 * (u // HEAD_GROUPS), 2 * (u // HEAD_GROUPS) + 1)

        FILLS = {3: (0, 2, 4), 4: (6, 8, 10), 5: (12, 14)}

        with nc.Block() as block:
            @block.tensor
            def _(pe):
                def transpose_norm(b):
                    pe.wait_ge(norm_ready, b + 1)
                    wait(pe, fill_done, MAX_FILLS * b)
                    for t in range(TILES):
                        last = nc.tensor.transpose(work_ps[0][:, 0, t * P:(t + 1) * P], normed[:, t, :],
                                                   s.ident32[:, :])
                    last.then_inc(normt_ps, 1)

                def project(b):
                    pe.wait_ge(normt_ready, b + 1)
                    for k, w in enumerate((s.wq_pairs, s.wk_pairs)):
                        for pair in range(2):
                            last = nc.tensor.matmul(work_ps[k][:, pair, :],
                                                    w[:, 2 * pair:2 * pair + 2, :, :].rearrange("d t r c -> d (t r c)"),
                                                    normed_t[:, :], start=True, stop=True)
                        last.then_inc(proj_ready, 1)

                def project_values(b):
                    wait(pe, shared, 2 * b - 3)
                    for t in range(TILES):
                        last = nc.tensor.matmul(turn_ps[:, t * P:(t + 1) * P], normed_t[:, t * P:(t + 1) * P],
                                                s.wv[:, :], start=True, stop=True)
                    last.then_inc(v_ready, 1)

                def feature_product(b, k):
                    pe.wait_ge(squares_ready, 2 * b + 2)
                    wait(pe, feat_ready, 2 * b + k)
                    for pair in range(2):
                        for half in range(2):
                            rows = slice(2 * GROUP * half, 2 * GROUP * (half + 1))
                            last = nc.tensor.matmul(work_ps[half][:, pair, :], s.feature_w[rows, pair, :],
                                                    with_square[k][rows, pair, :], start=True, stop=True)
                    last.then_inc(feat_ps, 1)

                def max_fill(b, parity, f):
                    tile, (group, tiles) = f // HEAD_UNITS, heads_of(f % HEAD_UNITS)
                    rows = slice(GROUP * group, GROUP * (group + 1))
                    if f == 0:
                        pe.wait_ge(parts_ready, 2 * b + 2)
                    if f >= 2:
                        pe.wait_ge(fill_done, MAX_FILLS * b + f - 1)
                    for n, t in enumerate(tiles):
                        last = nc.tensor.matmul(work_ps[f % 2][:, n, :], q1[parity][rows, t, tile * P:(tile + 1) * P],
                                                k1[parity][rows, t, :], start=True, stop=True)
                    last.then_inc(fill_ready, 1)

                def transpose_negmax(b, tile):
                    pe.wait_ge(fill_done, MAX_FILLS * b + HEAD_UNITS * (tile + 1))
                    if tile == 0:
                        pe.wait_ge(values_ready, b + 1)
                        wait(pe, mixedt_ready, b - 1)
                    else:
                        pe.wait_ge(shift_ready, TILES * b + tile)
                        wait(pe, added, b - 1)
                    for t in range(FTILES):
                        last = nc.tensor.matmul(turn_ps[:, t * P:(t + 1) * P], s.neg_max[:, tile, t, :],
                                                s.ident16[:, :], start=True, stop=True)
                    last.then_inc(negmax_ps, 1)

                def logits(b, parity, u):
                    n = HEAD_UNITS * b + u
                    if u == 0:
                        pe.wait_ge(shift_ready, TILES * (b + 1))
                    wait(pe, exp_done, n - 1)
                    group, tiles = heads_of(u)
                    rows = slice(GROUP * group, GROUP * (group + 1))
                    for key_tile in range(TILES):
                        keys = slice(key_tile * P, (key_tile + 1) * P)
                        for h, t in enumerate(tiles):
                            out = logits_ps[u % 2][:, key_tile, h, :]
                            nc.tensor.matmul(out, k1[parity][rows, t, keys], q1[parity][rows, t, :],
                                             start=True, stop=False)
                            last = nc.tensor.matmul(out, k2[parity][rows, t, keys], q2[parity][rows, t, :],
                                                    start=False, stop=True)
                    last.then_inc(logits_ready, 1)

                def mix(b, parity, u):
                    pe.wait_ge(low_ready, HEAD_UNITS * b + u + 1)
                    if u % HEAD_GROUPS == 0:
                        wait(pe, parts_kept, 2 * b + u // HEAD_GROUPS)
                    group, tiles = heads_of(u)
                    rows = slice(GROUP * group, GROUP * (group + 1))
                    for h, t in enumerate(tiles):
                        head = HEAD_GROUPS * t + group
                        steps = [(key_tile, part) for key_tile in range(TILES) for part in (probs_hi, probs_lo)]
                        for key_tile, part in steps:
                            last = nc.tensor.matmul(mixed_ps[rows, h, :], s.values[:, parity, key_tile, head, :],
                                                    part[u % PROB_BUFFERS][:, key_tile, h, :],
                                                    start=((key_tile, part) == steps[0]),
                                                    stop=((key_tile, part) == steps[-1]))
                    last.then_inc(pv_done, 1)

                def turn_parts(b, half, last_values=False):
                    pe.wait_ge(parts_kept, 2 * b + half + 1)
                    pe.wait_ge(values_ready, SAMPLES if last_values else b + half + 2)
                    if half == 0:
                        wait(pe, added, b)
                    else:
                        pe.wait_ge(shared, 2 * b + 1)
                    for tile in range(TILES):
                        for t in range(2):
                            n = 2 * tile + t
                            last = nc.tensor.transpose(turn_ps[:, n * P:(n + 1) * P],
                                                       mixed_parts[half][:, t, tile * P:(tile + 1) * P],
                                                       s.ident32[:, :])
                    last.then_inc(parts_turned, 1)

                def transpose_mixed(b):
                    pe.wait_ge(shared, 2 * b + 2)
                    for tile in range(TILES):
                        last = nc.tensor.transpose(turn_ps[:, tile * P:(tile + 1) * P],
                                                   mixed[:, tile, :, :].rearrange("p h c -> p (h c)"), s.ident32[:, :])
                    last.then_inc(mixedt_ps, 1)

                def output(b, preparing=True):
                    pe.wait_ge(mixedt_ready, b + 1)
                    if preparing:
                        pe.wait_ge(shift_ready, TILES * (b + 2) + 1)
                    for tile in range(TILES):
                        at = slice(tile * P, (tile + 1) * P)
                        last = nc.tensor.matmul(turn_ps[:, at], mixed_t[:, at], s.wo[:, :], start=True, stop=True)
                    last.then_inc(out_ready, 1)

                def fills(b, parity, u, part):
                    for first in FILLS.get(u, ())[part:part + 1]:
                        for f in range(first, first + 2):
                            max_fill(b, parity, f)

                def slot(b, parity, is_first=False, has_next=True, has_second=True):
                    for u in range(HEAD_UNITS):
                        if has_next:
                            fills(b + 1, 1 - parity, u, 0)
                        if has_second and u == 7:
                            project(b + 2)
                        if u < HEAD_UNITS - 1:
                            logits(b, parity, u + 1)
                        elif has_next:
                            logits(b + 1, 1 - parity, 0)
                        if has_second and u == 6:
                            transpose_norm(b + 2)
                        if has_next:
                            fills(b + 1, 1 - parity, u, 1)
                        if u > 0:
                            mix(b, parity, u - 1)
                        elif not is_first:
                            mix(b - 1, 1 - parity, HEAD_UNITS - 1)
                        if has_next:
                            if u == 0:
                                project_values(b + 1)
                            if u < 2:
                                feature_product(b + 1, u)
                            fills(b + 1, 1 - parity, u, 2)
                            if u in (4, 6):
                                transpose_negmax(b + 1, (u - 4) // 2)
                        if not is_first:
                            if u == 2:
                                turn_parts(b - 1, 1, not has_next)
                            elif u == 3:
                                transpose_mixed(b - 1)
                            elif u == 5:
                                output(b - 1, has_next)
                        if u == 7:
                            turn_parts(b, 0, not has_next)

                transpose_norm(0)
                project(0)
                project_values(0)
                for k in range(2):
                    feature_product(0, k)
                for u in range(2, 6):
                    for part in range(3):
                        fills(0, 0, u, part)
                    if u >= 4:
                        transpose_negmax(0, u - 4)
                transpose_norm(1)
                project(1)
                logits(0, 0, 0)
                slot(0, 0, is_first=True)
                with pairs(pe, 1, SAMPLES - 3) as i:
                    slot(i, 1)
                    slot(i + 1, 0)
                slot(SAMPLES - 3, 1)
                slot(SAMPLES - 2, 0, has_second=False)
                slot(SAMPLES - 1, 1, has_next=False, has_second=False)
                mix(SAMPLES - 1, 1, HEAD_UNITS - 1)
                turn_parts(SAMPLES - 1, 1, True)
                transpose_mixed(SAMPLES - 1)
                output(SAMPLES - 1, False)

            @block.scalar
            def _(act):
                def exps(b, u):
                    n = HEAD_UNITS * b + u
                    act.wait_ge(logits_ready, n + 1)
                    wait(act, pv_done, n - PROB_BUFFERS + 1)
                    nc.scalar.activation(probs_hi[u % PROB_BUFFERS][:, :, :, :], logits_ps[u % 2][:, :, :, :],
                                         ACT.Exp, bias=s.prob_shift[:, :])
                    wait(act, low_ready, n - 1)
                    nc.scalar.activation(probs[u % 2][:, :, :, :], logits_ps[u % 2][:, :, :, :],
                                         ACT.Exp, bias=s.prob_shift[:, :]).then_inc(exp_done, 1)

                def keep_mixed(b, half):
                    act.wait_ge(pv_done, HEAD_UNITS * b + HEAD_GROUPS * (half + 1))
                    wait(act, parts_turned, 2 * b + half - 1)
                    nc.scalar.activation(mixed_parts[half][:, :, :], mixed_ps[:, :, :], ACT.Copy).then_inc(parts_kept, 1)

                def keep_normed(b):
                    act.wait_ge(normt_ps, b + 1)
                    wait(act, v_ready, b)
                    nc.scalar.activation(normed_t[:, :], work_ps[0][:, 0, :], ACT.Copy).then_inc(normt_ready, 1)

                def mask(b):
                    for k in range(2):
                        act.wait_ge(proj_ready, 2 * b + k + 1)
                        wait(act, squares_ready, 2 * b + k - 1)
                        nc.scalar.activation(masks[k][:, :, :], work_ps[k][:, :, :], ACT.Identity,
                                             bias=s.linear_rows[:, :],
                                             scale=s.square_rows[:, :]).then_inc(masks_ready, 1)

                def feature(b, k):
                    act.wait_ge(feat_ps, 2 * b + k + 1)
                    wait(act, parts_ready, 2 * b + k - 1)
                    for t in range(FTILES):
                        last = nc.scalar.activation(features[k][:, t, :], work_ps[t % 2][:, t // 2, :], ACT.Exp,
                                                    bias=s.feature_bias[:, k * FTILES + t:k * FTILES + t + 1])
                    last.then_inc(feat_ready, 1)

                def keep_mixed_t(b):
                    act.wait_ge(mixedt_ps, b + 1)
                    wait(act, out_ready, b)
                    nc.scalar.activation(mixed_t[:, :], turn_ps[:, 0:TOKENS], ACT.Copy).then_inc(mixedt_ready, 1)

                def slot(b, is_first=False, has_next=True, has_second=True):
                    for u in range(HEAD_UNITS):
                        if u == 1 and not is_first:
                            keep_mixed(b - 1, 1)
                        if u == 5:
                            keep_mixed(b, 0)
                        if has_second and u == 7:
                            mask(b + 2)
                        exps(b, u)
                        if has_next and u < 2:
                            feature(b + 1, u)
                        if u == 3 and not is_first:
                            keep_mixed_t(b - 1)
                        if has_second and u == 6:
                            keep_normed(b + 2)

                keep_normed(0)
                mask(0)
                for k in range(2):
                    feature(0, k)
                keep_normed(1)
                mask(1)
                slot(0, is_first=True)
                with act.Fori(1, SAMPLES - 2, 1) as i:
                    slot(i)
                slot(SAMPLES - 2, has_second=False)
                slot(SAMPLES - 1, has_next=False, has_second=False)
                keep_mixed(SAMPLES - 1, 1)
                keep_mixed_t(SAMPLES - 1)

            @block.vector
            def _(dve):
                def apply(b, parity):
                    wait(dve, normt_ps, b)
                    norm.apply(dve, b, parity, normed)

                def split_values(b, parity):
                    dve.wait_ge(v_ready, b + 1)
                    wait(dve, pv_done, HEAD_UNITS * (b - 1))
                    wait(dve, values_ready, b)
                    link = Chain(dve, link_values, VALUE_PARTS * b)
                    v = turn_ps[:, 0:TOKENS].rearrange("p (t h c) -> p t h c", t=TILES, h=HEADS)
                    high, mid, low = (s.values[:, parity, :, :, n * HEAD_DIM:(n + 1) * HEAD_DIM]
                                      for n in range(VALUE_PARTS))
                    link(nc.vector.tensor_copy(high, v))
                    link(nc.vector.tensor_tensor(value_rest[:, :, :, :], v, high, ALU.subtract))
                    link(nc.vector.tensor_copy(mid, value_rest[:, :, :, :]))
                    nc.vector.tensor_tensor(low, value_rest[:, :, :, :], mid,
                                            ALU.subtract).then_inc(values_ready, 1)

                def square(b):
                    for k in range(2):
                        dve.wait_ge(masks_ready, 2 * b + k + 1)
                        wait(dve, feat_ps, 2 * b + k - 1)
                        nc.vector.tensor_tensor(with_square[k][:, :, :], masks[k][:, :, :], work_ps[k][:, :, :],
                                                ALU.mult).then_inc(squares_ready, 1)

                def split_queries(b, parity):
                    link = Chain(dve, link_parts, 2 * b)
                    dve.wait_ge(feat_ready, 2 * b + 1)
                    link(nc.vector.tensor_copy(q1[parity][:, :, :], features[0][:, :, :]))
                    nc.vector.tensor_tensor(q_low[:, :, :], features[0][:, :, :], q1[parity][:, :, :],
                                            ALU.subtract).then_inc(parts_ready, 1)

                def split_keys(b, parity):
                    link = Chain(dve, link_parts, 2 * b + 1)
                    dve.wait_ge(feat_ready, 2 * b + 2)
                    link(nc.vector.tensor_copy(k_high[:, :, :], features[1][:, :, :]))
                    nc.vector.tensor_scalar(k2[parity][:, :, :], k_high[:, :, :], s.first_copy[:, :],
                                            s.shift_row[:, :], ALU.mult, ALU.add)
                    nc.vector.scalar_tensor_tensor(k1[parity][:, :, :], k_high[:, :, :], s.minus_second[:, :],
                                                   features[1][:, :, :], ALU.mult, ALU.add).then_inc(parts_ready, 1)

                def maxima(b, u):
                    for f in [first + n for first in FILLS.get(u, ()) for n in range(2)]:
                        tile, (group, tiles) = f // HEAD_UNITS, heads_of(f % HEAD_UNITS)
                        dve.wait_ge(fill_ready, MAX_FILLS * b + f + 1)
                        if f % HEAD_UNITS == 0:
                            wait(dve, negmax_ps, TILES * b + tile - 1)
                        nc.vector.tensor_reduce(
                            s.neg_max[:, tile, tiles[0]:tiles[1] + 1, GROUP * group + SPLATS],
                            work_ps[f % 2][:, :, :], AX.X, ALU.max, negate=True).then_inc(fill_done, 1)

                def shift(b, parity, tile):
                    dve.wait_ge(negmax_ps, TILES * b + tile + 1)
                    at = slice(tile * P, (tile + 1) * P)
                    nc.vector.scalar_tensor_tensor(
                        q2[parity][:, :, at], q_low[:, :, at], s.first_copy[:, :],
                        turn_ps[:, :].rearrange("p (t i) -> p t i", t=FTILES),
                        ALU.mult, ALU.add).then_inc(shift_ready, 1)

                def share(b, half):
                    dve.wait_ge(parts_turned, 2 * b + half + 1)
                    link = Chain(dve, link_out, 2 * b + half)
                    parts = turn_ps[:, :].rearrange("p (n c) -> p n c", c=GROUP)
                    nc.vector.tensor_reduce(summed[:, :, :, :].rearrange("p t h c -> p (t h) c"),
                                            parts[:, :, 0:SUM_COLUMN].rearrange("p n (v c) -> p n c v", v=VALUE_PARTS),
                                            AX.X, ALU.add)
                    link(nc.vector.reciprocal(inverse[:, :, :].rearrange("p t h -> p (t h)"), parts[:, :, SUM_COLUMN]))
                    nc.vector.tensor_tensor(mixed[:, :, half * HEAD_UNITS:(half + 1) * HEAD_UNITS, :],
                                            summed[:, :, :, :],
                                            inverse[:, :, :].unsqueeze(3).to_broadcast([P, TILES, HEAD_UNITS, HEAD_DIM]),
                                            ALU.mult).then_inc(shared, 1)

                def add(b):
                    dve.wait_ge(out_ready, b + 1)
                    rows = tile_of(s.x_res, b)
                    nc.vector.tensor_tensor(rows, rows, turn_ps[:, 0:TOKENS].rearrange("p (t d) -> p t d", t=TILES),
                                            ALU.add).then_inc(added, 1)

                def slot(b, parity, is_first=False, has_next=True, has_second=True):
                    for u in range(HEAD_UNITS):
                        if has_next:
                            if u == 0:
                                split_values(b + 1, 1 - parity)
                                split_queries(b + 1, 1 - parity)
                            elif u == 1:
                                split_keys(b + 1, 1 - parity)
                            elif u < 6:
                                maxima(b + 1, u)
                            if u in (4, 6):
                                shift(b + 1, 1 - parity, (u - 4) // 2)
                        if not is_first:
                            if u == 2:
                                share(b - 1, 1)
                            elif u == 5:
                                add(b - 1)
                        if has_second:
                            if u == 1:
                                norm.statistics(dve, b + 2, parity)
                            elif u == 5:
                                apply(b + 2, parity)
                            elif u == 7:
                                square(b + 2)
                        if u == 7:
                            share(b, 0)

                norm.statistics(dve, 0, 0)
                apply(0, 0)
                norm.statistics(dve, 1, 1)
                square(0)
                split_values(0, 0)
                split_queries(0, 0)
                split_keys(0, 0)
                for u in range(2, 6):
                    maxima(0, u)
                    if u >= 4:
                        shift(0, 0, u - 4)
                apply(1, 1)
                square(1)
                slot(0, 0, is_first=True)
                with pairs(dve, 1, SAMPLES - 3) as i:
                    slot(i, 1)
                    slot(i + 1, 0)
                slot(SAMPLES - 3, 1)
                slot(SAMPLES - 2, 0, has_second=False)
                slot(SAMPLES - 1, 1, has_next=False, has_second=False)
                share(SAMPLES - 1, 1)
                add(SAMPLES - 1)

            @block.gpsimd
            def _(pool):
                def slot(b, parity, has_second=True):
                    for u in range(HEAD_UNITS):
                        n = HEAD_UNITS * b + u
                        if has_second and u == 4:
                            norm.power(pool, b + 2, parity)
                        pool.wait_ge(exp_done, n + 1)
                        wait(pool, pv_done, n - PROB_BUFFERS + 1)
                        nc.gpsimd.tensor_tensor(probs_lo[u % PROB_BUFFERS][:, :, :, :], probs[u % 2][:, :, :, :],
                                                probs_hi[u % PROB_BUFFERS][:, :, :, :],
                                                ALU.subtract).then_inc(low_ready, 1)

                norm.power(pool, 0, 0)
                norm.power(pool, 1, 1)
                slot(0, 0)
                with pairs(pool, 1, SAMPLES - 3) as i:
                    slot(i, 1)
                    slot(i + 1, 0)
                slot(SAMPLES - 3, 1)
                slot(SAMPLES - 2, 0, has_second=False)
                slot(SAMPLES - 1, 1, has_second=False)


def splines(nc, s, stage, out=None):
    with ExitStack() as ctx:
        sb, ps, sem = sb_maker(nc, ctx), ps_maker(nc, ctx), sem_maker(nc, ctx, stage)
        norm = RowNorm(nc, s, ctx, stage, 2)
        normed, norm_ready = norm.out, norm.ready
        normed_t = [sb(f"{stage}_normed_t{i}", [P, TOKENS], F32) for i in range(2)]
        bent = [sb(f"{stage}_bent{i}", [P, HALF_KNOTS, TOKENS], F32) for i in range(2)]
        turned = [ps(f"{stage}_turned{i}", [P, 512]) for i in range(2)]
        inner = [ps(f"{stage}_inner{i}", [P, 512]) for i in range(2)]
        result = [ps(f"{stage}_result{i}", [P, 512]) for i in range(2)]
        turned_ready, normt_ready, inner_ready, bent_ready, result_ready, biased, added, stored = (
            sem(n) for n in ("turned_ready", "normt_ready", "inner_ready", "bent_ready", "result_ready", "biased",
                             "added", "stored"))

        with nc.Block() as block:
            @block.vector
            def _(dve):
                def apply(b, parity):
                    wait(dve, turned_ready, b - 1)
                    norm.apply(dve, b, parity, normed[parity])

                def add(b, parity):
                    dve.wait_ge(result_ready, b + 1)
                    dve.wait_ge(biased, b + 1)
                    rows = tile_of(s.x_res, b)
                    nc.vector.tensor_tensor(rows, rows,
                                            result[parity][:, 0:TOKENS].rearrange("p (t d) -> p t d", t=TILES),
                                            ALU.add).then_inc(added, 1)

                norm.statistics(dve, 0, 0)
                norm.statistics(dve, 1, 1)
                apply(0, 0)
                apply(1, 1)
                norm.statistics(dve, 2, 0)
                apply(2, 0)
                norm.statistics(dve, 3, 1)
                add(0, 0)
                with pairs(dve, 1, SAMPLES - 3) as i:
                    for step, parity in ((0, 1), (1, 0)):
                        apply(i + step + 2, parity)
                        norm.statistics(dve, i + step + 3, 1 - parity)
                        add(i + step, parity)
                apply(SAMPLES - 1, 1)
                for b in range(SAMPLES - 3, SAMPLES):
                    add(b, b % 2)

            @block.gpsimd
            def _(pool):
                def bias(b):
                    wait(pool, norm_ready, b + 1)
                    rows = tile_of(s.x_res, b)
                    nc.gpsimd.tensor_tensor(rows, rows, s.half_bias[:, :, :], ALU.add).then_inc(biased, 1)

                norm.powers(pool, after=bias)

            @block.tensor
            def _(pe):
                def prepare(b, parity):
                    pe.wait_ge(norm_ready, b + 1)
                    wait(pe, normt_ready, b - 1)
                    for t in range(TILES):
                        last = nc.tensor.transpose(turned[parity][:, t * P:(t + 1) * P],
                                                   normed[parity][:, t, :], s.ident32[:, :])
                    last.then_inc(turned_ready, 1)

                def enter(b, parity):
                    pe.wait_ge(normt_ready, b + 1)
                    wait(pe, bent_ready, b - 1)
                    nc.tensor.matmul(inner[parity][:, 0:TOKENS], s.win2[:, :], normed_t[parity][:, :],
                                     start=True, stop=True).then_inc(inner_ready, 1)

                def leave(b, parity):
                    pe.wait_ge(bent_ready, b + 1)
                    wait(pe, added, b - 1)
                    for t in range(TILES):
                        for k in range(HALF_KNOTS):
                            last = nc.tensor.matmul(result[parity][:, t * P:(t + 1) * P],
                                                    bent[parity][:, k, t * P:(t + 1) * P], s.knot_out[:, k, :],
                                                    start=(k == 0), stop=(k == HALF_KNOTS - 1))
                    last.then_inc(result_ready, 1)

                prepare(0, 0)
                prepare(1, 1)
                enter(0, 0)
                prepare(2, 0)
                enter(1, 1)
                leave(0, 0)
                with pairs(pe, 1, SAMPLES - 3) as i:
                    for step, parity in ((0, 1), (1, 0)):
                        prepare(i + step + 2, parity)
                        enter(i + step + 1, 1 - parity)
                        leave(i + step, parity)
                prepare(SAMPLES - 1, 1)
                enter(SAMPLES - 2, 0)
                leave(SAMPLES - 3, 1)
                enter(SAMPLES - 1, 1)
                leave(SAMPLES - 2, 0)
                leave(SAMPLES - 1, 1)

            @block.scalar
            def _(act):
                def copy(b, parity):
                    act.wait_ge(turned_ready, b + 1)
                    wait(act, inner_ready, b - 1)
                    nc.scalar.activation(normed_t[parity][:, :], turned[parity][:, 0:TOKENS],
                                         ACT.Copy).then_inc(normt_ready, 1)

                def bend(b, parity):
                    act.wait_ge(inner_ready, b + 1)
                    wait(act, result_ready, b - 1)
                    for k in range(HALF_KNOTS):
                        last = nc.scalar.activation(bent[parity][:, k, :], inner[parity][:, 0:TOKENS], ACT.Relu,
                                                    bias=s.relu_bias[:, k:k + 1], scale=s.relu_scale[:, k:k + 1])
                    last.then_inc(bent_ready, 1)

                copy(0, 0)
                copy(1, 1)
                bend(0, 0)
                with pairs(act, 1, SAMPLES - 1) as i:
                    for step, parity in ((0, 1), (1, 0)):
                        copy(i + step + 1, 1 - parity)
                        bend(i + step, parity)
                bend(SAMPLES - 1, 1)

            if out is not None:
                @block.sync
                def _(sp):
                    rows = out.rearrange("b (t p) d -> p (b t) d", p=P)
                    with sp.Fori(0, SAMPLES, 1) as b:
                        sp.wait_ge(added, b + 1)
                        sp.dma_start(rows[:, bass.ds(b * TILES, TILES), :], tile_of(s.x_res, b)).then_inc(stored, 16)
                    sp.wait_ge(stored, 16 * SAMPLES)


def causal_attention(nc, s, stage):
    BLOCKS = ((0, 0), (1, 0), (1, 1))
    with ExitStack() as ctx:
        sb, ps, sem = sb_maker(nc, ctx), ps_maker(nc, ctx), sem_maker(nc, ctx, stage)
        norm = RowNorm(nc, s, ctx, stage, 1)
        normed, norm_ready = norm.out[0], norm.ready
        normed_t = sb(stage + "_normed_t", [P, TOKENS], F32)
        qk = [sb(f"{stage}_qk{i}", [P, 2, TOKENS], F32) for i in range(2)]
        v = [sb(f"{stage}_v{i}", [P, TILES, P], F32) for i in range(2)]
        masked = sb(stage + "_masked", [P, 3 * P], F32)
        neg_max = sb(stage + "_neg_max", [P, TILES], F32)
        probs = [sb(f"{stage}_probs{i}", [P, 3 * P], F32) for i in range(2)]
        sums = [sb(f"{stage}_sums{i}", [P, TILES], F32) for i in range(2)]
        inverse = [sb(f"{stage}_inverse{i}", [P, TILES], F32) for i in range(2)]
        probs_t = sb(stage + "_probs_t", [P, 3 * P], F32)
        turn_ps = ps(stage + "_turn_ps", [P, 512])
        qk_ps = ps(stage + "_qk_ps", [P, 2, TOKENS])
        v_ps = ps(stage + "_v_ps", [P, 512])
        scores_ps = ps(stage + "_scores_ps", [P, 512])
        probst_ps = ps(stage + "_probst_ps", [P, 512])
        result_ps = ps(stage + "_result_ps", [P, 512])
        (turned, normt_ready, qk_done, v_done, qk_ready, v_ready, scores_done, masked_ready, max_ready,
         exp_done, probst_done, probst_ready, result_done, added, link_sum) = (
            sem(n) for n in ("turned", "normt_ready", "qk_done", "v_done", "qk_ready", "v_ready",
                             "scores_done", "masked_ready", "max_ready", "exp_done", "probst_done", "probst_ready",
                             "result_done", "added", "link_sum"))
        SCALE = 1.0 / math.sqrt(P)
        SPANS = (slice(0, P), slice(P, 3 * P))

        with nc.Block() as block:
            def run(engine, *steps):
                def turn(b, parity):
                    for step, lead in steps:
                        if not isinstance(b, int) or 0 <= b + lead < SAMPLES:
                            step(b + lead, (parity + lead) % 2)

                for b in range(-2, 2):
                    turn(b, b % 2)
                with pairs(engine, 2, SAMPLES - 4) as i:
                    turn(i, 0)
                    turn(i + 1, 1)
                for b in range(SAMPLES - 4, SAMPLES):
                    turn(b, b % 2)

            @block.vector
            def _(dve):
                def projections(b, parity):
                    wait(dve, turned, b)
                    norm.apply(dve, b, parity, normed)
                    if not (isinstance(b, int) and b + 1 >= SAMPLES):
                        norm.statistics(dve, b + 1, 1 - parity)

                def values(b, parity):
                    dve.wait_ge(v_done, b + 1)
                    wait(dve, result_done, b - 1)
                    nc.vector.tensor_tensor(v[parity][:, :, :], v_ps[:, 0:TOKENS].rearrange("p (t c) -> p t c", t=TILES),
                                            s.attn1_bv[:, :].unsqueeze(1).to_broadcast([P, TILES, P]),
                                            ALU.add).then_inc(v_ready, 1)

                def scores(b, parity):
                    dve.wait_ge(scores_done, b + 1)
                    wait(dve, exp_done, b)
                    nc.vector.scalar_tensor_tensor(masked[:, :], scores_ps[:, 0:3 * P], SCALE, s.causal[:, :],
                                                   ALU.mult, ALU.add).then_inc(masked_ready, 1)
                    dve.wait_ge(masked_ready, b + 1)
                    for t in range(TILES):
                        last = nc.vector.tensor_reduce(neg_max[:, t:t + 1], masked[:, SPANS[t]], AX.X, ALU.max,
                                                       negate=True)
                    last.then_inc(max_ready, 1)

                def result(b, parity):
                    link = Chain(dve, link_sum, b)
                    dve.wait_ge(exp_done, b + 1)
                    link(nc.vector.reciprocal(inverse[parity][:, :], sums[parity][:, :]))
                    dve.wait_ge(result_done, b + 1)
                    for t in range(TILES):
                        rows = tile_of(s.x_res, b, t)
                        last = nc.vector.scalar_tensor_tensor(rows, result_ps[:, t * P:(t + 1) * P],
                                                              inverse[parity][:, t:t + 1], rows, ALU.mult, ALU.add)
                    last.then_inc(added, 1)

                norm.statistics(dve, 0, 0)
                run(dve, (projections, 2), (result, 0), (values, 2), (scores, 1))

            @block.gpsimd
            def _(pool):
                norm.powers(pool)

            @block.tensor
            def _(pe):
                def projections(b, parity):
                    pe.wait_ge(norm_ready, b + 1)
                    wait(pe, normt_ready, b)
                    for t in range(TILES):
                        last = nc.tensor.transpose(turn_ps[:, t * P:(t + 1) * P], normed[:, t, :], s.ident32[:, :])
                    last.then_inc(turned, 1)
                    pe.wait_ge(normt_ready, b + 1)
                    wait(pe, v_ready, b)
                    for t in range(TILES):
                        last = nc.tensor.matmul(v_ps[:, t * P:(t + 1) * P], normed_t[:, t * P:(t + 1) * P],
                                                s.attn1_w[:, 2 * P:3 * P], start=True, stop=True)
                    last.then_inc(v_done, 1)
                    wait(pe, qk_ready, b)
                    for k in range(2):
                        last = nc.tensor.matmul(qk_ps[:, k, :], s.attn1_w[:, k * P:(k + 1) * P], normed_t[:, :],
                                                start=True, stop=True)
                    last.then_inc(qk_done, 1)

                def scores(b, parity):
                    pe.wait_ge(qk_ready, b + 1)
                    wait(pe, masked_ready, b)
                    for t in range(TILES):
                        last = nc.tensor.matmul(scores_ps[:, SPANS[t]], qk[parity][:, 0, t * P:(t + 1) * P],
                                                qk[parity][:, 1, 0:(t + 1) * P], start=True, stop=True)
                    last.then_inc(scores_done, 1)

                def turn_probs(b, parity):
                    pe.wait_ge(exp_done, b + 1)
                    wait(pe, probst_ready, b)
                    for n in range(len(BLOCKS)):
                        last = nc.tensor.transpose(probst_ps[:, n * P:(n + 1) * P],
                                                   probs[parity][:, n * P:(n + 1) * P], s.ident32[:, :])
                    last.then_inc(probst_done, 1)

                def result(b, parity):
                    pe.wait_ge(probst_ready, b + 1)
                    pe.wait_ge(v_ready, b + 1)
                    wait(pe, added, b)
                    for n, (tile, key_tile) in enumerate(BLOCKS):
                        last = nc.tensor.matmul(result_ps[:, tile * P:(tile + 1) * P], probs_t[:, n * P:(n + 1) * P],
                                                v[parity][:, key_tile, :], start=(key_tile == 0),
                                                stop=(key_tile == tile))
                    last.then_inc(result_done, 1)

                run(pe, (turn_probs, 0), (projections, 2), (result, 0), (scores, 1))

            @block.scalar
            def _(act):
                def projections(b, parity):
                    act.wait_ge(turned, b + 1)
                    wait(act, qk_done, b)
                    nc.scalar.activation(normed_t[:, :], turn_ps[:, 0:TOKENS], ACT.Copy).then_inc(normt_ready, 1)
                    act.wait_ge(qk_done, b + 1)
                    wait(act, scores_done, b - 1)
                    for k in range(2):
                        last = nc.scalar.activation(qk[parity][:, k, :], qk_ps[:, k, :], ACT.Identity,
                                                    bias=s.attn1_bqk[:, k:k + 1])
                    last.then_inc(qk_ready, 1)

                def scores(b, parity):
                    act.wait_ge(max_ready, b + 1)
                    wait(act, probst_done, b - 1)
                    for t in range(TILES):
                        last = nc.scalar.activation(probs[parity][:, SPANS[t]], masked[:, SPANS[t]], ACT.Exp,
                                                    bias=neg_max[:, t:t + 1], accum_out=sums[parity][:, t:t + 1])
                    last.then_inc(exp_done, 1)

                def result(b, parity):
                    act.wait_ge(probst_done, b + 1)
                    wait(act, result_done, b)
                    nc.scalar.activation(probs_t[:, :], probst_ps[:, 0:3 * P], ACT.Copy).then_inc(probst_ready, 1)

                run(act, (result, 0), (projections, 2), (scores, 1))


def build(nc, a, out):
    with ExitStack() as ctx:
        sb = sb_maker(nc, ctx)
        s = Store()
        s.x_loaded = ctx.enter_context(nc.semaphore("x_loaded"))
        s.x_res = sb("x_res", [P, SAMPLES * TILES, P], F32)
        s.norm_hi = sb("norm_hi", [P, SAMPLES, TOKENS], F16)
        s.norm_lo = sb("norm_lo", [P, SAMPLES, TOKENS], F16)
        s.pooled = sb("pooled", [P, SAMPLES], F32)
        s.ident32 = sb("ident32", [P, P], F32)
        s.ident16 = sb("ident16", [P, P], F16)
        s.causal = sb("causal", [P, 3 * P], F32)
        s.row_index = sb("row_index", [P, 1], I32)
        s.ones_row = sb("ones_row", [1, P], F32)
        s.eps = sb("eps", [P, TILES], F32)
        s.minus_half = sb("minus_half", [P, TILES], F32)
        s.wa_hi, s.wa_lo, s.wb_hi, s.wb_lo = (
            sb(name, [P, ZONES * ZONE_HIDDEN], F16) for name in ("wa_hi", "wa_lo", "wb_hi", "wb_lo"))
        s.router_w1 = sb("router_w1", [P, ROUTER_H], F32)
        s.router_w2 = sb("router_w2", [ROUTER_H, ZONES], F32)
        s.router_b1 = sb("router_b1", [ROUTER_H, 1], F32)
        s.router_b2 = sb("router_b2", [1, ZONES], F32)
        s.zone_code = sb("zone_code", [1, SAMPLES], U32)
        s.unit_scale = sb("unit_scale", [P, UNITS], F32)
        s.gelu_scale = sb("gelu_scale", [P, 1], F32)
        s.hidden_scale = sb("hidden_scale", [P, 1], F32)
        s.zone_out_scale = sb("zone_out_scale", [P, 1], F32)
        s.wq_pairs = sb("wq_pairs", [P, FTILES, 2, GROUP], F32)
        s.wk_pairs = sb("wk_pairs", [P, FTILES, 2, GROUP], F32)
        s.wv = sb("wv", [P, P], F32)
        s.wo = sb("wo", [P, P], F32)
        s.feature_w = sb("feature_w", [P, 2, P], F32)
        s.feature_bias = sb("feature_bias", [P, 2 * FTILES], F32)
        s.first_copy = sb("first_copy", [P, 1], F32)
        s.minus_second = sb("minus_second", [P, 1], F32)
        s.shift_row = sb("shift_row", [P, 1], F32)
        s.linear_rows = sb("linear_rows", [P, 1], F32)
        s.square_rows = sb("square_rows", [P, 1], F32)
        s.neg_max = sb("neg_max", [P, TILES, FTILES, P], F16)
        s.values = sb("values", [P, 2, TILES, HEADS, GROUP], BF16)
        s.prob_shift = sb("prob_shift", [P, 1], F32)
        s.attn1_w = sb("attn1_w", [P, 3 * P], F32)
        s.attn1_bqk = sb("attn1_bqk", [P, 2], F32)
        s.attn1_bv = sb("attn1_bv", [P, P], F32)
        s.win2 = sb("win2", [P, P], F32)
        s.relu_scale = sb("relu_scale", [P, HALF_KNOTS], F32)
        s.relu_bias = sb("relu_bias", [P, HALF_KNOTS], F32)
        s.knot_out = sb("knot_out", [P, HALF_KNOTS, P], F32)
        s.half_bias = sb("half_bias", [P, TILES, P], F32)

        with ExitStack() as setup:
            st = sb_maker(nc, setup)
            s.stage_a = st("stage_a", [P, ZONES * ZONE_HIDDEN], F32)
            s.stage_b = st("stage_b", [P, ZONES * ZONE_HIDDEN], F32)
            s.qkv_rows = st("qkv_rows", [P, 3, P], F32)
            s.out_rows = st("out_rows", [P, P], F32)
            s.centers = st("centers", [P, SPLATS], F32)
            s.deltas = st("deltas", [P, SPLATS], F32)
            s.log_scales = st("log_scales", [P, SPLATS], F32)
            s.log_amps = st("log_amps", [P, SPLATS], F32)
            s.movement = st("movement", [P, 1], F32)
            s.temperature = st("temperature", [P, 1], F32)
            s.bin2 = st("bin2", [P, 1], F32)
            s.knot_b1 = st("knot_b1", [P, HALF_KNOTS], F32)
            s.knot_w2 = st("knot_w2", [P, HALF_KNOTS], F32)
            s.wout2 = st("wout2", [P, P], F32)
            s.b2_col = st("b2_col", [SPLINES, 1], F32)
            s.bout_row = st("bout_row", [1, P], F32)
            load_and_constants(nc, s, a)
            prepare_zones(nc, s)
            prepare_splats(nc, s)
            prepare_splines(nc, s)

        zone_norm(nc, s, "norm_a")
        route(nc, s, "route_a")
        zones(nc, s, "zones_a")
        splat_attention(nc, s, "splat")
        zone_norm(nc, s, "norm_b")
        route(nc, s, "route_b")
        zones(nc, s, "zones_b")
        splines(nc, s, "spline_a")
        causal_attention(nc, s, "causal")
        splines(nc, s, "spline_b", out)


INPUTS = ["L0_attn_x", "L0_attn_splat_centers", "L0_attn_splat_deltas", "L0_attn_splat_log_scales",
          "L0_attn_splat_log_amplitudes", "L0_attn_movement_scale", "L0_attn_temperature", "L0_attn_qkv_w",
          "L0_attn_out_w", "L0_ffn_W1", "L0_ffn_b1", "L0_ffn_W2", "L0_ffn_b2", "L0_ffn_Wa", "L0_ffn_Wb",
          "L1_attn_W", "L1_attn_b", "L1_ffn_Win", "L1_ffn_bin_", "L1_ffn_W1", "L1_ffn_b1", "L1_ffn_W2",
          "L1_ffn_b2", "L1_ffn_Wout", "L1_ffn_bout"]


def kernel(**inputs):
    import numpy as np
    import concourse.bacc as bacc
    from concourse.bass_utils import run_bass_kernel_spmd

    nc = bacc.Bacc("TRN2", target_bir_lowering=False, num_devices=1)
    arrays, aps = {}, {}
    for name in INPUTS:
        array = np.ascontiguousarray(inputs[name])
        if array.ndim == 0:
            array = array.reshape(1)
        arrays[name] = array
        aps[name] = nc.dram_tensor(name, array.shape, mybir.dt.from_np(array.dtype), kind="ExternalInput").ap()
    out = nc.dram_tensor("out", (SAMPLES, TOKENS, P), F32, kind="ExternalOutput").ap()
    build(nc, aps, out)
    results = run_bass_kernel_spmd(nc, [arrays], core_ids=[0])
    return results.results[0]["out"]
```
